# Optimizing a Trainium2 kernel written in Bass

```python
import numpy as np
import jax
import jax.numpy as jnp

def _softmax(x, axis=-1):
    return jax.nn.softmax(x, axis=axis)

def _gelu(x):
    return jax.nn.gelu(x, approximate=True)

def _silu(x):
    return jax.nn.silu(x)

def _sigmoid(x):
    return jax.nn.sigmoid(x)

def _layernorm(x, axis=-1, eps=1e-05):
    m = jnp.mean(x, axis=axis, keepdims=True)
    v = jnp.var(x, axis=axis, keepdims=True)
    return (x - m) / jnp.sqrt(v + eps)

def _scatter_add(tgt, idx, src, axis=0):
    return tgt.at[idx].add(src)

def _segment_sum(src, seg, n):
    return jax.ops.segment_sum(src, seg, n)
kernel_name = 'mk_prb_d1_jaxref_r4_0d889c'

def setup_inputs(seed: int=0):
    np.random.seed(seed)
    _w = jnp.asarray

    def _L0_attn_setup():
        import jax, jax.numpy as jnp
        import numpy as np
        B, S, E, H = (2, 512, 512, 16)
        NOPE, ROPE, VD = (128, 64, 128)
        QH = NOPE + ROPE
        LORA = 128
        ROPE_THETA = 10000.0
        EPS = 1e-06

        def _rope(xp, cos, sin):
            d2 = xp.shape[-1] // 2
            x1, x2 = (xp[..., :d2], xp[..., d2:])
            return jnp.concatenate([x1 * cos - x2 * sin, x2 * cos + x1 * sin], axis=-1)
        key = jax.random.key(seed)
        ks = jax.random.split(key, 5)
        sd = lambda n: 1.0 / np.sqrt(n)
        return {'x': jax.random.normal(ks[0], (B, S, E), jnp.float32), 'wq': jax.random.normal(ks[1], (E, H * QH), jnp.float32) * sd(E), 'wkv_a': jax.random.normal(ks[2], (E, LORA + ROPE), jnp.float32) * sd(E), 'wkv_b': jax.random.normal(ks[3], (LORA, H * (NOPE + VD)), jnp.float32) * sd(LORA), 'wo': jax.random.normal(ks[4], (H * VD, E), jnp.float32) * sd(H * VD), 'kv_norm_scale': jnp.ones((LORA,), jnp.float32)}
    _L0_attn_in = _L0_attn_setup()

    def _L0_ffn_setup():
        import math
        import jax, jax.numpy as jnp
        import numpy as np
        DIM = 512
        RANK = 8
        B, T = (4, 1024)

        def _orthogonal(key, n):
            a = jax.random.normal(key, (n, n), dtype=jnp.float32)
            q, r = jnp.linalg.qr(a)
            q = q * jnp.sign(jnp.diagonal(r))[None, :]
            return q
        key = jax.random.key(seed)
        kx, kf = jax.random.split(key)
        x = jax.random.normal(kx, (B, T, DIM), dtype=jnp.float32)
        fkeys = jax.random.split(kf, RANK)
        factors = jnp.stack([_orthogonal(fkeys[r], DIM) * (r + 1) ** (-0.5) for r in range(RANK)])
        bias = jnp.zeros((DIM,), dtype=jnp.float32)
        return {'x': x, 'factors': factors, 'bias': bias}
    _L0_ffn_in = _L0_ffn_setup()
    _d = {'L0_attn_x': _L0_attn_in['x'], 'L0_attn_wq': _L0_attn_in['wq'], 'L0_attn_wkv_a': _L0_attn_in['wkv_a'], 'L0_attn_wkv_b': _L0_attn_in['wkv_b'], 'L0_attn_wo': _L0_attn_in['wo'], 'L0_attn_kv_norm_scale': _L0_attn_in['kv_norm_scale'], 'L0_ffn_factors': _L0_ffn_in['factors'], 'L0_ffn_bias': _L0_ffn_in['bias']}
    _x0 = _d['L0_attn_x']
    _d['L0_attn_x'] = jax.random.normal(jax.random.fold_in(jax.random.key(seed), 1), (1, 2048, 512), dtype=_x0.dtype)
    del _x0
    return _d

def reference(L0_attn_x, L0_attn_wq, L0_attn_wkv_a, L0_attn_wkv_b, L0_attn_wo, L0_attn_kv_norm_scale, L0_ffn_factors, L0_ffn_bias):

    def _L0_attn_ref(x, wq, wkv_a, wkv_b, wo, kv_norm_scale):
        import jax, jax.numpy as jnp
        import numpy as np
        B, S, E, H = (2, 512, 512, 16)
        NOPE, ROPE, VD = (128, 64, 128)
        QH = NOPE + ROPE
        LORA = 128
        ROPE_THETA = 10000.0
        EPS = 1e-06

        def _rope(xp, cos, sin):
            d2 = xp.shape[-1] // 2
            x1, x2 = (xp[..., :d2], xp[..., d2:])
            return jnp.concatenate([x1 * cos - x2 * sin, x2 * cos + x1 * sin], axis=-1)
        b, s, _ = x.shape
        q = (x @ wq).reshape(b, s, H, QH).transpose(0, 2, 1, 3)
        q_nope, q_pe = (q[..., :NOPE], q[..., NOPE:])
        kva = x @ wkv_a
        ckv, k_pe = (kva[..., :LORA], kva[..., LORA:])
        ckv = ckv * jax.lax.rsqrt(jnp.mean(ckv * ckv, axis=-1, keepdims=True) + EPS)
        ckv = ckv * kv_norm_scale
        kv = (ckv @ wkv_b).reshape(b, s, H, NOPE + VD).transpose(0, 2, 1, 3)
        k_nope, v = (kv[..., :NOPE], kv[..., NOPE:])
        pos = jnp.arange(s, dtype=jnp.float32)
        inv = 1.0 / ROPE_THETA ** (jnp.arange(0, ROPE, 2, dtype=jnp.float32) / ROPE)
        ang = pos[:, None] * inv
        cos, sin = (jnp.cos(ang), jnp.sin(ang))
        q_pe = _rope(q_pe, cos, sin)
        k_pe = _rope(k_pe[:, None, :, :], cos, sin)
        qs = jnp.concatenate([q_nope, q_pe], axis=-1)
        ks_ = jnp.concatenate([k_nope, jnp.broadcast_to(k_pe, (b, H, s, ROPE))], axis=-1)
        scale = QH ** (-0.5)
        scores = jnp.einsum('bhqd,bhkd->bhqk', qs, ks_) * scale
        causal = jnp.tril(jnp.ones((s, s), dtype=bool))
        scores = jnp.where(causal, scores, jnp.finfo(scores.dtype).min)
        attn = jax.nn.softmax(scores, axis=-1)
        out = jnp.einsum('bhqk,bhkd->bhqd', attn, v)
        out = out.transpose(0, 2, 1, 3).reshape(b, s, H * VD)
        return out @ wo

    def _L0_ffn_ref(x, factors, bias):
        import math
        import jax, jax.numpy as jnp
        import numpy as np
        DIM = 512
        RANK = 8
        B, T = (4, 1024)

        def _orthogonal(key, n):
            a = jax.random.normal(key, (n, n), dtype=jnp.float32)
            q, r = jnp.linalg.qr(a)
            q = q * jnp.sign(jnp.diagonal(r))[None, :]
            return q
        rank = factors.shape[0]
        mixed = jnp.einsum('btd,rde->bte', x, factors)
        mixed = mixed / math.sqrt(rank) + bias
        return mixed
    x = L0_attn_x
    xn = _layernorm(x, axis=-1)
    x = x + _L0_attn_ref(xn, L0_attn_wq, L0_attn_wkv_a, L0_attn_wkv_b, L0_attn_wo, L0_attn_kv_norm_scale) + _L0_ffn_ref(xn, L0_ffn_factors, L0_ffn_bias)
    return x

_drawn_inputs = setup_inputs


def setup_inputs(seed=0):
    import zlib

    import numpy as np

    out = dict(_drawn_inputs(seed))
    spreads = {'L0_attn_kv_norm_scale': (1.0, 0.2), 'L0_ffn_bias': (0.0, 0.1)}
    factors = {}
    for name, (base, spread) in spreads.items():
        noise = np.random.default_rng([zlib.crc32(name.encode()), seed]).standard_normal(out[name].shape)
        drawn = base * np.exp(spread * noise) if base else spread * noise
        out[name] = jnp.asarray(drawn.astype(out[name].dtype))
    for name, factor in factors.items():
        out[name] = (out[name] * factor).astype(out[name].dtype)
    return out
```

```python
from contextlib import ExitStack

import numpy as np
import concourse.bass as bass
from concourse import mybir

F32, F32R = mybir.dt.float32, mybir.dt.float32r
F16, BF16 = mybir.dt.float16, mybir.dt.bfloat16
ALU = mybir.AluOpType
ACT = mybir.ActivationFunctionType
AX_X = mybir.AxisListType.X

P = 128
S, E, H = 2048, 512, 16
NOPE, ROPE, VD, LORA, RANK = 128, 64, 128, 128, 8
QH, HALF = NOPE + ROPE, ROPE // 2
CH = 512
NT, NC, KE, QT = S // P, S // CH, E // P, CH // P
SCALE = QH ** -0.5
FIRST = [sum(QT * (i + 1) for i in range(c)) for c in range(NC + 1)]
HT = FIRST[NC]
BT = 2 * HT
LAG, AHEAD = 2, 22
NB = H // 2
NEG = -1.0e30
HEADROOM = float(np.log(32.0)) / SCALE
PERIOD = {"tile": BT, "unit": 2 * NC, "head": 2}


def where(tile):
    h, s = divmod(tile, HT)
    c = max(c for c in range(NC) if FIRST[c] <= s)
    return h, c, s - FIRST[c], h * NC + c


class Silent:
    def then_inc(self, *a, **k):
        return self
    matmul = transpose = activation = tensor_copy = tensor_tensor = tensor_scalar = then_inc
    tensor_reduce = tensor_tensor_reduce = scalar_tensor_tensor = reciprocal = memset = then_inc
    bn_stats = bn_aggr = affine_select = dma_start = wait_ge = then_inc


class Counts:

    def __init__(self, sems):
        self.sems = sems
        self.at = {(part, s): {} for part in ("pre", "body", "last") for s in sems}
        self.total = {k: 0 for k in self.at}
        self.dry, self.part, self.it, self.seen, self.own = True, None, 0, {}, None

    def bias(self, s):
        return max(0, self.total["body", s] - self.total["pre", s])

    def begin(self, part, it):
        self.part, self.it, self.seen = part, it, {}

    def inc(self, ins, s, key, n=1):
        if self.dry:
            self.total[self.part, s] += n
            self.at[self.part, s][key] = self.total[self.part, s]
        ins.then_inc(self.sems[s], n)

    def wait(self, eng, s, key):
        if self.dry:
            return
        name, scope, index = key[:3]
        earlier = (name, scope, index + PERIOD[scope]) + tuple(key[3:])
        pre, body = self.total["pre", s], self.total["body", s]
        here = self.at[self.part, s]
        if self.part == "pre":
            if key not in here:
                raise KeyError((s, key))
            offset, done = self.bias(s), here[key]
        else:
            offset = self.bias(s) + pre
            if key in here:
                done = here[key]
            elif earlier in self.at["body", s]:
                done = self.at["body", s][earlier] - body
            else:
                raise KeyError((self.part, s, key))
        if self.seen.get(s, -10 ** 9) >= done:
            return
        self.seen[s] = done
        if self.part == "body":
            eng.wait_ge(self.sems[s], self.it * body + (offset + done))
            if self.own:
                eng.sem_inc(self.own, 1)
        else:
            eng.wait_ge(self.sems[s], offset + done + (body * (NB - 1) if self.part == "last" else 0))

    def wait_all(self, eng, part):
        for s in self.sems:
            n = self.bias(s) + self.total["pre", s]
            if part == "last":
                n += body_n(self, s)
            if n:
                eng.wait_ge(self.sems[s], n)


def body_n(counts, s):
    return counts.total["body", s] * (NB - 1) + counts.total["last", s]


def build(nc, x, wq, wkv_a, wkv_b, wo, kvs, factors, bias, rope_t, rope_n, out):
    ctx = ExitStack()
    with ctx:
        def sb(name, shape, dt):
            return ctx.enter_context(nc.sbuf_tensor(name, shape, dt))

        xTh = sb("xTh", [P, KE, S], F32R)
        xTl = sb("xTl", [P, KE, S], F32R)
        kTh = sb("kTh", [P, S], F32R)
        kTl = sb("kTl", [P, S], F32R)
        kR4 = sb("kR4", [P, S], F32R)
        kR5 = sb("kR5", [P, S], F32R)
        vH = sb("vH", [P, NT, LORA], F16)
        vL = sb("vL", [P, NT, LORA], F16)
        acc = sb("acc", [P, NT, E], F32)
        q = sb("q", [P, NC, 4, CH], F32R)
        wAbs = [sb(f"wAbs{i}", [P, KE, LORA], F32R) for i in range(2)]
        wPe = [sb(f"wPe{i}", [P, KE, P], F32R) for i in range(2)]
        wVo = [sb(f"wVo{i}", [P, E], F32R) for i in range(2)]
        wX = [sb(f"wX{i}", [P, KE, P], F32R) for i in range(2)]
        wKT = [sb(f"wKT{i}", [P, LORA], F32R) for i in range(2)]
        wVT = [sb(f"wVT{i}", [P, LORA], F32R) for i in range(2)]
        wst = sb("wst", [P, KE, P], F32)
        wkv = sb("wkv", [P, 2 * P], F32)
        tab = sb("tab", [P, 2, CH], F32)
        ex = sb("ex", [P, 2, CH], F32)
        pH = sb("pH", [P, 4, CH], F16)
        pL = sb("pL", [P, 4, CH], F16)
        esum = sb("esum", [P, 2, CH], F32)
        oH = sb("oH", [P, CH], F32R)
        oL = sb("oL", [P, CH], F32R)
        junk = sb("junk", [P, CH], BF16)
        gmax = sb("gmax", [P, NC, QT * NC], F32)
        rmax = sb("rmax", [P, 2, QT], F32)
        rden = sb("rden", [P, QT], F32)
        ident = sb("ident", [P, P], F32)
        identr = sb("identr", [P, P], F32R)
        upper = sb("upper", [P, P], F32R)
        cmask = sb("cmask", [P, CH], BF16)
        ones = sb("ones", [P, 1], F32)
        eps = sb("eps", [P, 2], F32)
        scl = sb("scl", [P, 1], F32)
        ropen = sb("ropen", [P, NT, 2, HALF], F32)
        stats = sb("stats", [P, NT, 6], F32)
        mv = sb("mv", [P, NT, 2], F32)
        rstd = sb("rstd", [P, 2, NT], F32)
        ssq = sb("ssq", [P, 3, NT], F32)
        ps = ctx.enter_context(nc.psum_tensor("ps", [P, 8, CH], F32))
        SB, GB, OB, MB = 0, 2, 4, 6

        wa_f = pH[:, :, :].rearrange("p a n -> p (a n)").bitcast(F32)[:, 0:KE * QH].rearrange(
            "p (k n) -> p k n", k=KE)
        fsumA = pH[:, :, :].rearrange("p a n -> p (a n)").bitcast(F32).rearrange("p (k n) -> p k n", k=2)
        fsumB = pL[:, :, :].rearrange("p a n -> p (a n)").bitcast(F32).rearrange("p (k n) -> p k n", k=2)
        fsum = [fsumA[:, 0, :], fsumA[:, 1, :], fsumB[:, 0, :], fsumB[:, 1, :]]
        wa = [q[:, i, :, :].rearrange("p a n -> p (a n)")[:, 0:KE * QH].rearrange("p (k n) -> p k n", k=KE)
              for i in range(2)]
        ff = [q[:, 2 + i, :, :] for i in range(2)]
        kt = [tab[:, i, :].rearrange("p (t n) -> p t n", t=2) for i in range(2)]
        biasb = wst[:, :, :].rearrange("p k n -> p (k n)")
        umask = wkv[:, 0:P]
        ktmp = wkv[:, P:2 * P].rearrange("p (a t n) -> p a t n", a=2, t=2)
        stash = nc.dram_tensor("rope_stash", [NC, 2, P, CH], F32).ap()

        names = ["S", "G", "PV", "M",
                 "exp", "hi", "Ph",
                 "sum", "max", "free",
                 "Pl", "pool",
                 "d_wst", "d_wkv", "d_tab", "d_x", "d_w", "d_c", "d_f0", "d_f1", "d_stash", "d_out"]
        names += [f"d_q{c}" for c in range(NC)]
        sems = {n: ctx.enter_context(nc.semaphore("s_" + n)) for n in names}
        cn = Counts(sems)
        idle = {w: ctx.enter_context(nc.semaphore("idle_" + w)) for w in ("dve", "sp")}
        wait, inc = cn.wait, cn.inc
        misc = {"n": 0}

        def f(ap):
            return ap.bitcast(F32)

        def three(e, o, a, b, first=True, last=True):
            e.matmul(o, a[0], b[0], start=first, stop=False)
            e.matmul(o, a[0], b[1], start=False, stop=False)
            return e.matmul(o, a[1], b[0], start=False, stop=last)

        def bank(e, who, key, previous):
            n = misc["n"]
            misc["n"] += 1
            if who == "pe" and previous[n % 2] is not None:
                wait(e, "free", previous[n % 2])
            previous[n % 2] = key
            return ps[:, MB + n % 2, :]

        prev = {"v": [None, None]}

        def split(e, who, key, src, hi, lo):
            if who == "act":
                wait(e, "M", key)
                inc(e.activation(hi, src, ACT.Copy), "hi", key)
            if who == "dve":
                wait(e, "hi", key)
                inc(e.tensor_tensor(lo, src, f(hi), ALU.subtract), "free", key)

        def constants(e, who):
            k = ("const", "unit", 0)
            if who == "pool":
                e.memset(ones[:, :], 1.0)
                e.memset(eps[:, 0:1], 1e-5)
                e.memset(eps[:, 1:2], 1e-6)
                e.memset(cmask[:, :], 0.0)
                e.memset(umask, 0.0)
                inc(e.memset(ident[:, :], 0.0), "pool", ("zero", "unit", 0))
                wait(e, "pool", ("zero", "unit", 0))
                e.affine_select(out=ident[:, :], in_=ident[:, :], compare_op=ALU.not_equal, fill=1.0,
                                base=0, pattern=[[-1, P]], channel_multiplier=1)
                e.affine_select(out=cmask[:, :], in_=cmask[:, :], compare_op=ALU.is_ge, fill=NEG,
                                base=CH - P, pattern=[[-1, CH]], channel_multiplier=1)
                inc(e.affine_select(out=umask, in_=umask, compare_op=ALU.is_ge, fill=NEG,
                                    base=0, pattern=[[1, P]], channel_multiplier=-1), "pool", k)
            if who == "dve":
                e.memset(f(kR5[HALF * 2:HALF * 3, :]), 1.0)
                wait(e, "pool", k)
                e.tensor_copy(identr[:, :], ident[:, :])
                inc(e.tensor_copy(upper[:, :], umask), "free", k)

        def first_loads(e, who):
            k = ("ld", "unit", 0)
            if who == "sp":
                e.dma_start(acc[:, 0:QT, :], x[0:CH, :].rearrange("(t p) n -> p t n", p=P)) \
                    .then_inc(sems["d_x"], 16)
                cn_add("d_x", ("x", "unit", 0), 16)
                inc(e.dma_start(wa_f, wkv_a.rearrange("(k p) n -> p k n", p=P)), "d_w", k, 16)
                for c in range(1, NC):
                    wait(e, "d_x", ("x", "unit", c - 1))
                    inc(e.dma_start(acc[:, QT * c:QT * c + QT, :],
                                    x[CH * c:CH * c + CH, :].rearrange("(t p) n -> p t n", p=P)),
                        "d_x", ("x", "unit", c), 16)
                    if c == 1:
                        e.dma_start(ropen[:, :, :, :], rope_n).then_inc(sems["d_c"], 16)
                        e.dma_start(scl[:, :], kvs.rearrange("(p a) -> p a", a=1)).then_inc(sems["d_c"], 16)
                        cn_add("d_c", k, 32)
                        inc(e.dma_start(biasb, bias.rearrange("(a n) -> a n", a=1).broadcast_to([P, E])
                                        ), "d_c", k, 16)

        def cn_add(s, key, n):
            if cn.dry:
                cn.total[cn.part, s] += n
                cn.at[cn.part, s][key] = cn.total[cn.part, s]

        def split_wa(e, who):
            k = ("wa", "unit", 0)
            if who == "act":
                wait(e, "d_w", ("ld", "unit", 0))
                inc(e.activation(wa[0], wa_f, ACT.Copy), "hi", k)
            if who == "dve":
                wait(e, "hi", k)
                inc(e.tensor_tensor(wa[1], wa_f, f(wa[0]), ALU.subtract), "free", k)

        def norm_stats(e, who, c):
            ts = slice(QT * c, QT * c + QT)
            if who == "dve":
                wait(e, "d_x", ("x", "unit", c))
                for t in range(QT * c, QT * c + QT):
                    ins = e.bn_stats(stats[:, t, :], acc[:, t, :])
                inc(ins, "free", ("bn", "unit", c))
                wait(e, "free", ("bn", "unit", c))
                for t in range(QT * c, QT * c + QT):
                    ins = e.bn_aggr(mv[:, t, :], stats[:, t, :])
                inc(ins, "free", ("var", "unit", c))
                wait(e, "hi", ("sd", "unit", c))
                inc(e.reciprocal(rstd[:, 1, ts], rstd[:, 0, ts]), "free", ("rstd", "unit", c))
            if who == "act":
                wait(e, "pool", ("const", "unit", 0))
                wait(e, "free", ("var", "unit", c))
                inc(e.activation(rstd[:, 0, ts], mv[:, ts, 1], ACT.Sqrt, bias=eps[:, 0:1]), "hi",
                    ("sd", "unit", c))

        def transpose_x(e, who, t):
            k = ("xt", "unit", t)
            b = bank(e, who, k, prev["v"])
            xn = esum[:, t % 2, :]
            if who == "dve":
                wait(e, "free", ("rstd", "unit", t // QT))
                if t >= 2:
                    wait(e, "M", ("xt", "unit", t - 2))
                inc(e.tensor_scalar(xn, acc[:, t, :], mv[:, t, 0:1], rstd[:, 1, t:t + 1],
                                    ALU.subtract, ALU.mult), "free", ("xn", "unit", t))
            if who == "pe":
                wait(e, "pool", ("const", "unit", 0))
                wait(e, "free", ("xn", "unit", t))
                for k4 in range(KE):
                    ins = e.transpose(b[:, k4 * P:(k4 + 1) * P], xn[:, k4 * P:(k4 + 1) * P], ident[:, :])
                inc(ins, "M", k)
            if who == "pool":
                wait(e, "d_c", ("ld", "unit", 0))
                wait(e, "free", ("xn", "unit", t))
                inc(e.tensor_tensor(acc[:, t, :], acc[:, t, :], biasb, ALU.add), "pool",
                    ("bias", "unit", t))
            cols = slice(t * P, t * P + P)
            split(e, who, k, b.rearrange("p (k n) -> p k n", k=KE), xTh[:, :, cols], xTl[:, :, cols])

        def latent(e, who, p2):
            k = ("kva", "unit", p2)
            b = bank(e, who, k, prev["v"])[:, 0:2 * QH].rearrange("p (t n) -> p t n", t=2)
            ts = slice(2 * p2, 2 * p2 + 2)
            cos, sin = ropen[:, ts, 0, :], ropen[:, ts, 1, :]
            lo, hi = b[:, :, LORA:LORA + HALF], b[:, :, LORA + HALF:QH]
            kk = kt[p2 % 2]
            r1, r2 = kk[:, :, LORA:LORA + HALF], kk[:, :, LORA + HALF:LORA + ROPE]
            if who == "pe":
                wait(e, "free", ("wa", "unit", 0))
                wait(e, "free", ("xt", "unit", 2 * p2 + 1))
                for i in range(2):
                    cols = slice((2 * p2 + i) * P, (2 * p2 + i + 1) * P)
                    for k4 in range(KE):
                        ins = three(e, b[:, i, :], [xTh[:, k4, cols], xTl[:, k4, cols]],
                                    [wa[0][:, k4, :], wa[1][:, k4, :]], k4 == 0, k4 == KE - 1)
                inc(ins, "M", k)
            if who == "act":
                wait(e, "M", k)
                for i in range(2):
                    if 2 * p2 + i:
                        wait(e, "hi", ("sq", "unit", 2 * p2 + i - 1))
                    inc(e.activation(junk[:, 0:LORA], b[:, i, 0:LORA], ACT.Square,
                                     accum_out=ssq[:, 0, 2 * p2 + i:2 * p2 + i + 1]), "hi",
                        ("sq", "unit", 2 * p2 + i))
                wait(e, "hi", ("sq", "unit", 2 * p2 + 1))
                inc(e.activation(ssq[:, 1, ts], ssq[:, 0, ts], ACT.Sqrt, bias=eps[:, 1:2],
                                 scale=1.0 / LORA), "hi", ("rms", "unit", p2))
            if who == "dve":
                wait(e, "d_c", ("ld", "unit", 0))
                wait(e, "hi", ("rms", "unit", p2))
                inc(e.reciprocal(ssq[:, 2, ts], ssq[:, 1, ts]), "free", ("rr", "unit", p2))
                if p2 >= 2:
                    wait(e, "M", ("kT", "unit", p2 - 2))
                    wait(e, "pool", ("vL", "unit", p2 - 2))
                wait(e, "free", ("rr", "unit", p2))
                for i in range(2):
                    e.tensor_scalar(kk[:, i, 0:LORA], b[:, i, 0:LORA], ssq[:, 2, 2 * p2 + i:2 * p2 + i + 1],
                                    None, ALU.mult)
                e.tensor_tensor(r1, lo, cos, ALU.mult)
                e.tensor_tensor(ktmp[:, 0, :, :], hi, sin, ALU.mult)
                e.tensor_tensor(r2, hi, cos, ALU.mult)
                inc(e.tensor_tensor(ktmp[:, 1, :, :], lo, sin, ALU.mult), "free", k)
                wait(e, "free", k)
                e.tensor_tensor(r1, r1, ktmp[:, 0, :, :], ALU.subtract)
                inc(e.tensor_tensor(r2, r2, ktmp[:, 1, :, :], ALU.add), "free", ("rope", "unit", p2))
                wait(e, "free", ("rope", "unit", p2))
                inc(e.tensor_copy(kk[:, :, LORA + ROPE:2 * P], kk[:, :, LORA:LORA + ROPE]), "free",
                    ("kk", "unit", p2))

        def keys(e, who, p2):
            k = ("kT", "unit", p2)
            b = bank(e, who, k, prev["v"])
            kk = kt[p2 % 2]
            cols = slice(2 * p2 * P, (2 * p2 + 2) * P)
            if who == "pe":
                wait(e, "free", ("kk", "unit", p2))
                for i in range(2):
                    e.transpose(b[:, i * P:(i + 1) * P], kk[:, i, 0:P], ident[:, :])
                    ins = e.transpose(b[:, (2 + i) * P:(3 + i) * P], kk[:, i, P:2 * P], ident[:, :])
                inc(ins, "M", k)
            if who == "act":
                wait(e, "free", ("kk", "unit", p2))
                inc(e.activation(vH[:, 2 * p2:2 * p2 + 2, :], kk[:, :, 0:LORA], ACT.Copy), "hi",
                    ("vH", "unit", p2))
                wait(e, "M", k)
                e.activation(kTh[:, cols], b[:, 0:2 * P], ACT.Copy)
                inc(e.activation(kR4[:, cols], b[:, 2 * P:4 * P], ACT.Copy), "hi", k)
            if who == "pool":
                wait(e, "hi", ("vH", "unit", p2))
                inc(e.tensor_tensor(vL[:, 2 * p2:2 * p2 + 2, :], kk[:, :, 0:LORA],
                                    vH[:, 2 * p2:2 * p2 + 2, :], ALU.subtract), "pool", ("vL", "unit", p2))
            if who == "dve":
                wait(e, "hi", k)
                e.tensor_tensor(kTl[:, cols], b[:, 0:2 * P], f(kTh[:, cols]), ALU.subtract)
                inc(e.tensor_tensor(kR5[0:ROPE, cols], b[0:ROPE, 2 * P:4 * P], f(kR4[0:ROPE, cols]),
                                    ALU.subtract), "free", k)

        def factor(e, who, i):
            r, k4 = divmod(i, KE)
            k = ("fac", "unit", i)
            src = factors[r, k4 * P:(k4 + 1) * P, :]
            if r == 0:
                if who == "sp":
                    wait(e, "free", ("wa", "unit", 0))
                    ins = e.dma_start(fsum[k4], src)
                    ins.then_inc(sems["d_w"], 16)
                    cn_add("d_w", k, 16)
                return
            if who == "sp":
                if i >= KE + 2:
                    wait(e, "pool", ("fac", "unit", i - 2))
                inc(e.dma_start(ex[:, i % 2, :], src), f"d_f{i % 2}", k, 16)
            if who == "pool":
                wait(e, "d_w", ("fac", "unit", KE - 1))
                wait(e, f"d_f{i % 2}", k)
                if r > 1:
                    wait(e, "pool", ("fac", "unit", i - KE))
                inc(e.tensor_tensor(fsum[k4], fsum[k4], ex[:, i % 2, :], ALU.add), "pool", k)

        def split_ff(e, who):
            for k4 in range(KE):
                k = ("ff", "unit", k4)
                if who == "act":
                    wait(e, "pool", ("fac", "unit", RANK * KE - KE + k4))
                    inc(e.activation(ff[0][:, k4, :], fsum[k4], ACT.Copy), "hi", k)
                if who == "dve":
                    wait(e, "hi", k)
                    inc(e.tensor_tensor(ff[1][:, k4, :], fsum[k4], f(ff[0][:, k4, :]), ALU.subtract),
                        "free", k)

        def ffn(e, who, t):
            k = ("ffn", "unit", t)
            b = bank(e, who, k, prev["v"])
            cols = slice(t * P, t * P + P)
            if who == "pe":
                wait(e, "free", ("xt", "unit", t))
                wait(e, "free", ("ff", "unit", KE - 1))
                for k4 in range(KE):
                    ins = three(e, b, [xTh[:, k4, cols], xTl[:, k4, cols]],
                                [ff[0][:, k4, :], ff[1][:, k4, :]], k4 == 0, k4 == KE - 1)
                inc(ins, "M", k)
            if who == "dve":
                wait(e, "M", k)
                wait(e, "pool", ("bias", "unit", t))
                inc(e.scalar_tensor_tensor(out=acc[:, t, :], in0=b, scalar=float(RANK) ** -0.5,
                                           in1=acc[:, t, :], op0=ALU.mult, op1=ALU.add), "free", k)

        def head0():
            return cn.it * 2

        def load(e, who, kind, h, after):
            if who != "sp":
                return
            wait(e, after[0], after[1])
            k = ("w" + kind, "head", h)
            wqv = wq.rearrange("(k p) n -> p k n", p=P)
            hh = head0() + h
            if kind == "q":
                inc(e.dma_start(wst[:, :, :], wqv[:, :, bass.ds(hh * QH, NOPE)]), "d_wst", k, 16)
            if kind == "o":
                inc(e.dma_start(wst[:, :, :], wo[bass.ds(hh * VD, VD), :].rearrange(
                    "p (k n) -> p k n", k=KE)), "d_wst", k, 16)
            if kind == "pe":
                for half in range(2):
                    for b in range(2):
                        at = (2 * half + b) * HALF
                        ins = e.dma_start(wst[:, :, at:at + HALF],
                                          wqv[:, :, bass.ds(hh * QH + b * QH + NOPE + half * HALF, HALF)])
                        inc(ins, "d_wst", k, 16)

        def load_kv(e, who, h, first=False):
            if who == "sp":
                if first:
                    wait(e, "free", ("rope", "unit", NT // 2 - 1))
                else:
                    wait(e, "M", ("wvt", "head", h - 1))
                inc(e.dma_start(wkv[:, :], wkv_b[:, bass.ds((head0() + h) * 2 * P, 2 * P)]), "d_wkv",
                    ("wkv", "head", h), 16)
            if who == "dve":
                wait(e, "d_c", ("ld", "unit", 0)) if cn.part == "pre" else None
                wait(e, "d_wkv", ("wkv", "head", h))
                inc(e.tensor_scalar(wkv[:, :], wkv[:, :], scl[:, 0:1], None, ALU.mult), "free",
                    ("kvs", "head", h))

        def wq_transpose(e, who, h):
            k = ("tq", "head", h)
            b = bank(e, who, k, prev["v"])
            if who == "pe":
                wait(e, "d_wst", ("wq", "head", h))
                for k4 in range(KE):
                    ins = e.transpose(b[:, k4 * P:(k4 + 1) * P], wst[:, k4, :], ident[:, :])
                inc(ins, "M", k)
            if who == "act" and not (cn.part == "pre"):
                wait(e, "M", ("wvo", "head", h - 1))
            split(e, who, k, b.rearrange("p (k n) -> p k n", k=KE), wX[0][:, :, :], wX[1][:, :, :])

        def wk_transpose(e, who, h):
            k = ("tk", "head", h)
            b = bank(e, who, k, prev["v"])[:, 0:P]
            if who == "pe":
                wait(e, "free", ("kvs", "head", h))
                inc(e.transpose(b, wkv[:, 0:P], ident[:, :]), "M", k)
            split(e, who, k, b, wKT[0][:, :], wKT[1][:, :])

        def w_abs(e, who, h):
            k = ("wabs", "head", h)
            b = bank(e, who, k, prev["v"])
            if who == "pe":
                wait(e, "free", ("tq", "head", h))
                wait(e, "free", ("tk", "head", h))
                for k4 in range(KE):
                    ins = three(e, b[:, k4 * P:(k4 + 1) * P], [w[:, k4, :] for w in wX],
                                [w[:, :] for w in wKT])
                inc(ins, "M", k)
            split(e, who, k, b.rearrange("p (k n) -> p k n", k=KE), wAbs[0][:, :, :], wAbs[1][:, :, :])

        def w_pe(e, who, h):
            k = ("pew", "head", h)
            if who == "act":
                wait(e, "d_wst", ("wpe", "head", h))
                if cn.part != "pre":
                    wait(e, "M", ("pe", "unit", (h - 2) * NC + NC - 1))
                inc(e.activation(wPe[0][:, :, :], wst[:, :, :], ACT.Copy), "hi", k)
            if who == "dve":
                wait(e, "hi", k)
                inc(e.tensor_tensor(wPe[1][:, :, :], wst[:, :, :], f(wPe[0][:, :, :]), ALU.subtract),
                    "free", k)

        def wv_transpose(e, who, h):
            k = ("wvt", "head", h)
            b = bank(e, who, k, prev["v"])[:, 0:P]
            if who == "pe":
                wait(e, "free", ("kvs", "head", h))
                inc(e.transpose(b, wkv[:, P:2 * P], ident[:, :]), "M", k)
            split(e, who, k, b, wVT[0][:, :], wVT[1][:, :])

        def w_o(e, who, h):
            k = ("wos", "head", h)
            if who == "act":
                wait(e, "d_wst", ("wo", "head", h))
                wait(e, "M", ("wabs", "head", h) if cn.part == "pre" else ("wabs", "head", h))
                inc(e.activation(wX[0][:, :, :], wst[:, :, :], ACT.Copy), "hi", k)
            if who == "dve":
                wait(e, "hi", k)
                inc(e.tensor_tensor(wX[1][:, :, :], wst[:, :, :], f(wX[0][:, :, :]), ALU.subtract),
                    "free", k)

        def w_vo(e, who, h):
            k = ("wvo", "head", h)
            b = bank(e, who, k, prev["v"])
            if who == "pe":
                wait(e, "free", ("wos", "head", h))
                ins = three(e, b, [w[:, :] for w in wVT], [w[:, :, :].rearrange("p k n -> p (k n)") for w in wX])
                inc(ins, "M", k)
            split(e, who, k, b, wVo[0][:, :], wVo[1][:, :])

        def q_latent(e, who, u):
            h, c = divmod(u, NC)
            k = ("q", "unit", u)
            b = bank(e, who, k, prev["v"])
            cols = slice(c * CH, c * CH + CH)
            if who == "pe":
                wait(e, "free", ("wabs", "head", h))
                for k4 in range(KE):
                    ins = three(e, b, [w[:, k4, :] for w in wAbs], [xTh[:, k4, cols], xTl[:, k4, cols]],
                                k4 == 0, k4 == KE - 1)
                inc(ins, "M", k)
            if who == "act" and cn.part != "pre":
                wait(e, "S", last_tile(u - NC))
            split(e, who, k, b, q[:, c, 0, :], q[:, c, 1, :])

        def last_tile(u):
            h, c = divmod(u, NC)
            return ("s", "tile", h * HT + FIRST[c + 1] - 1)

        def load_table(e, who, u, *after):
            if who == "sp":
                for a in after:
                    wait(e, *a)
                c = u % NC
                inc(e.dma_start(tab[:, :, :], rope_t[:, :, c * CH:(c + 1) * CH]), "d_tab",
                    ("tab", "unit", u), 16)

        def q_rope(e, who, u):
            h, c = divmod(u, NC)
            k = ("pe", "unit", u)
            b = bank(e, who, k, prev["v"])
            cols = slice(c * CH, c * CH + CH)
            cos, sin = tab[:, 0, :], tab[:, 1, :]
            if who == "pe":
                wait(e, "free", ("pew", "head", h))
                for k4 in range(KE):
                    ins = three(e, b, [w[:, k4, :] for w in wPe], [xTh[:, k4, cols], xTl[:, k4, cols]],
                                k4 == 0, k4 == KE - 1)
                inc(ins, "M", k)
            if who == "dve":
                wait(e, "d_tab", ("tab", "unit", u))
                wait(e, "M", k)
                e.tensor_tensor(cos, b, cos, ALU.mult)
                e.tensor_tensor(sin[0:ROPE, :], b[ROPE:P, :], sin[0:ROPE, :], ALU.mult)
                inc(e.tensor_tensor(sin[ROPE:P, :], b[0:ROPE, :], sin[ROPE:P, :], ALU.mult), "free", k)
            if who == "pool":
                wait(e, "free", k)
                inc(e.tensor_tensor(cos, cos, sin, ALU.add), "pool", ("ro", "unit", u))
                wait(e, "hi", k)
                inc(e.tensor_tensor(cos, cos, sin, ALU.subtract), "pool", k)
            if who == "act":
                wait(e, "pool", ("ro", "unit", u))
                inc(e.activation(sin.bitcast(F32R), cos, ACT.Copy), "hi", k)
            if who == "sp":
                wait(e, "pool", k)
                if cn.part != "pre":
                    wait(e, f"d_q{c}", ("qr", "unit", u - NC))
                inc(e.dma_start(stash[c].rearrange("a p n -> p a n"), tab[:, :, :]), "d_stash", k, 16)
                if cn.part != "pre":
                    wait(e, "S", last_tile(u - NC))
                fill(e, u, [tab[:, i, :] for i in range(2)], 0)

        def fill(e, u, lohi, b):
            c = u % NC
            lo, hi = lohi
            for half in range(2):
                src = slice((2 * half + b) * HALF, (2 * half + b + 1) * HALF)
                dst = half * HALF
                e.dma_start(f(q[dst:dst + HALF, c, 2, :]), hi[src, :]).then_inc(sems[f"d_q{c}"], 16)
                e.dma_start(f(q[dst:dst + HALF, c, 3, :]), hi[src, :]).then_inc(sems[f"d_q{c}"], 16)
                cn_add(f"d_q{c}", None, 32)
                inc(e.dma_start(f(q[ROPE + dst:ROPE + dst + HALF, c, 2, :]), lo[src, :]), f"d_q{c}",
                    ("qr", "unit", u), 16)

        def q_rope_second(e, who, u):
            if who == "sp":
                wait(e, "d_stash", ("pe", "unit", u - NC))
                wait(e, "S", last_tile(u - NC))
                fill(e, u, [stash[u % NC, i] for i in range(2)], 1)

        def group(e, who, g):
            h, c, j, u = where(g)
            t, kg = divmod(j, c + 1)
            k = ("g", "tile", g)
            n = CH if kg < c else (t + 1) * P
            b = ps[:, GB + g % 2, 0:n]
            qs, ks = slice(t * P, t * P + P), slice(kg * CH, kg * CH + n)
            m = gmax[:, u % NC, t * NC + kg:t * NC + kg + 1]
            if who == "pe":
                if not (cn.part == "pre" and g < 2):
                    wait(e, "max", ("g", "tile", g - 2))
                if j == 0:
                    wait(e, "free", ("q", "unit", u))
                e.matmul(b, q[:, c, 0, qs], kTh[:, ks], start=True, stop=False)
                if j == 0:
                    wait(e, f"d_q{c}", ("qr", "unit", u))
                inc(e.matmul(b, q[0:ROPE, c, 2, qs], kR4[0:ROPE, ks], start=False, stop=True), "G", k)
            if who == "dve":
                if not (cn.part == "pre" and g < 1):
                    wait(e, "max", ("g", "tile", g - 1))
                wait(e, "G", k)
                if kg < c:
                    inc(e.tensor_reduce(m, b, AX_X, ALU.max), "max", k)
                else:
                    if cn.part == "body" and not cn.dry:
                        e.sem_inc(idle["dve"], 1)
                    inc(e.tensor_tensor_reduce(out=junk[:, 0:n], in0=b, in1=cmask[:, CH - n:CH], scale=1.0,
                                               scalar=NEG, op0=ALU.add, op1=ALU.max, accum_out=m), "max", k)

        def max_row(e, who, u):
            h, c = divmod(u, NC)
            k = ("mT", "unit", u)
            b = bank(e, who, k, prev["v"])[0:QT, 0:P]
            gm = gmax[:, u % NC, :].rearrange("p (t g) -> p t g", t=QT)[:, :, 0:c + 1]
            if who == "dve":
                wait(e, "max", ("g", "tile", h * HT + FIRST[c + 1] - 1))
                inc(e.tensor_reduce(rmax[:, 0, :], gm, AX_X, ALU.max), "free", ("rm", "unit", u))
                wait(e, "free", ("rm", "unit", u))
                inc(e.tensor_scalar(rmax[:, 1, :], rmax[:, 0, :], -1.0, HEADROOM, ALU.mult, ALU.add),
                    "free", ("nm", "unit", u))
                wait(e, "M", k)
                qq = q[ROPE:ROPE + QT, c, 3, :].rearrange("p (t n) -> p t n", t=QT)
                inc(e.tensor_tensor(qq, b.unsqueeze(1).broadcast_to([QT, QT, P]),
                                    ident[0:QT, 0:QT].unsqueeze(2).broadcast_to([QT, QT, P]), ALU.mult),
                    "free", k)
            if who == "pe":
                wait(e, "free", ("nm", "unit", u))
                inc(e.transpose(b, rmax[:, 1, :], ident[:, :]), "M", k)

        def scores(e, who, T):
            h, c, j, u = where(T)
            k = ("s", "tile", T)
            n0 = max(0, j - QT * c) * P
            b = ps[:, SB + T % 2, n0:CH]
            ks = slice(j * P, j * P + P)
            x2, x4 = T % 2, T % 4
            if who == "pe":
                if not (cn.part == "pre" and T < 2):
                    wait(e, "exp", ("s", "tile", T - 2))
                if j == 0:
                    wait(e, "free", ("mT", "unit", u))
                three(e, b, [kTh[:, ks], kTl[:, ks]], [q[:, c, 0, n0:], q[:, c, 1, n0:]], True, False)
                if j >= QT * c:
                    e.matmul(ps[:, SB + T % 2, n0:n0 + P], identr[:, :], upper[:, :], start=False, stop=False)
                e.matmul(b, kR4[:, ks], q[:, c, 2, n0:], start=False, stop=False)
                inc(e.matmul(b, kR5[0:ROPE + QT, ks], q[0:ROPE + QT, c, 3, n0:], start=False, stop=True),
                    "S", k)
            if who == "act":
                if not (cn.part == "pre" and T < 2):
                    wait(e, "sum", ("s", "tile", T - 2))
                    wait(e, "Pl", ("s", "tile", T - 2))
                wait(e, "S", k)
                inc(e.activation(ex[:, x2, n0:], b, ACT.Exp, scale=SCALE), "exp", k)
                if not (cn.part == "pre" and T < 4):
                    wait(e, "PV", ("s", "tile", T - 4))
                wait(e, "exp", k)
                inc(e.activation(pH[:, x4, n0:], ex[:, x2, n0:], ACT.Copy), "Ph", k)
            if who == "pool":
                wait(e, "Ph", k)
                inc(e.tensor_tensor(pL[:, x4, n0:], ex[:, x2, n0:], pH[:, x4, n0:], ALU.subtract), "Pl", k)

        def row_sum(e, who, T):
            h, c, j, u = where(T)
            n0 = max(0, j - QT * c) * P
            if who == "dve":
                k = ("s", "tile", T)
                wait(e, "exp", k)
                es = esum[:, u % 2, n0:]
                if j == 0:
                    inc(e.tensor_copy(es, ex[:, T % 2, n0:]), "sum", k)
                else:
                    wait(e, "sum", ("s", "tile", T - 1))
                    inc(e.tensor_tensor(es, es, ex[:, T % 2, n0:], ALU.add), "sum", k)

        def values(e, who, T):
            h, c, j, u = where(T)
            n0 = max(0, j - QT * c) * P
            if who == "pe":
                k = ("s", "tile", T)
                if j == 0:
                    wait(e, "free", ("o", "unit", u - 2))
                wait(e, "Pl", k)
                inc(three(e, ps[:, OB + u % 2, n0:], [vH[:, j, :], vL[:, j, :]],
                          [pH[:, T % 4, n0:], pL[:, T % 4, n0:]], j == 0, j == QT * (c + 1) - 1), "PV", k)

        def read_output(e, who, u):
            h, c = divmod(u, NC)
            k = ("o", "unit", u)
            b = ps[:, OB + u % 2, :]
            if who == "act":
                wait(e, "PV", ("s", "tile", h * HT + FIRST[c + 1] - 1))
                wait(e, "M", ("out", "unit", u - 1, QT - 1))
                inc(e.activation(oH[:, :], b, ACT.Copy), "hi", k)
            if who == "dve":
                wait(e, "hi", k)
                inc(e.tensor_tensor(oL[:, :], b, f(oH[:, :]), ALU.subtract), "free", k)

        def denominators(e, who, u):
            h, c = divmod(u, NC)
            k = ("den", "unit", u)
            b = bank(e, who, k, prev["v"])[:, 0:QT]
            if who == "pe":
                wait(e, "sum", ("s", "tile", h * HT + FIRST[c + 1] - 1))
                for t in range(QT):
                    ins = e.matmul(b[:, t:t + 1], esum[:, u % 2, t * P:(t + 1) * P], ones[:, :],
                                   start=True, stop=True)
                inc(ins, "M", k)
            if who == "dve":
                wait(e, "M", k)
                wait(e, "free", ("o", "unit", u))
                inc(e.reciprocal(rden[:, :], b), "free", k)

        def head_output(e, who, u, t):
            h, c = divmod(u, NC)
            k = ("out", "unit", u, t)
            b = bank(e, who, k, prev["v"])
            if who == "pe":
                wait(e, "free", ("o", "unit", u))
                wait(e, "free", ("wvo", "head", h))
                inc(three(e, b, [oH[:, t * P:(t + 1) * P], oL[:, t * P:(t + 1) * P]], [w[:, :] for w in wVo]),
                    "M", k)
            a = acc[:, QT * c + t, :]
            if who == "dve":
                wait(e, "M", k)
                wait(e, "free", ("den", "unit", u))
                inc(e.scalar_tensor_tensor(out=a, in0=b, scalar=rden[:, t:t + 1], in1=a, op0=ALU.mult,
                                           op1=ALU.add), "free", k)
            if who == "sp" and cn.part == "last" and h == 1:
                wait(e, "free", k)
                inc(e.dma_start(out[(QT * c + t) * P:(QT * c + t + 1) * P, :], a), "d_out", k, 16)

        def prologue():
            yield constants,
            yield first_loads,
            yield split_wa,
            for c in range(NC):
                yield norm_stats, c
                for t in range(QT * c, QT * c + QT):
                    yield transpose_x, t
                    for i in range(2 * t, 2 * t + 2):
                        yield factor, i
                for p2 in range(2 * c, 2 * c + 2):
                    yield latent, p2
                for p2 in range(2 * c, 2 * c + 2):
                    yield keys, p2
            yield split_ff,
            yield load, "q", 0, ("pool", ("bias", "unit", NT - 1))
            yield load_kv, 0, True
            for t in range(NT):
                yield ffn, t
            yield wq_transpose, 0
            yield load, "pe", 0, ("M", ("tq", "head", 0))
            yield wk_transpose, 0
            yield w_abs, 0
            yield w_pe, 0
            yield load, "o", 0, ("free", ("pew", "head", 0))
            yield load_table, 0, ("M", ("kT", "unit", NT // 2 - 1)), ("pool", ("vL", "unit", NT // 2 - 1))
            for c in range(NC):
                yield q_latent, c
                yield q_rope, c
                yield load_table, c + 1 if c < NC - 1 else 2 * NC, (f"d_q{c}", ("qr", "unit", c))
            yield w_o, 0
            yield wv_transpose, 0
            yield load, "q", 1, ("free", ("wos", "head", 0))
            yield load_kv, 1
            for g in range(AHEAD):
                yield group, g
                for u in range(2):
                    if g == FIRST[u + 1]:
                        yield max_row, u
            for T in range(LAG):
                yield scores, T
            yield row_sum, 0

        def slots(last):
            for T in range(BT):
                h, c, j, u = where(T)
                s = T % HT
                more = not last or h == 0
                yield values, T
                if not last or T + LAG < BT:
                    yield scores, T + LAG
                if not last or T + AHEAD < BT:
                    yield group, T + AHEAD
                if not last or T + 1 < BT:
                    yield row_sum, T + 1
                for uu in range(2, 2 * NC + 2):
                    hh, cc = divmod(uu, NC)
                    if hh * HT + FIRST[cc + 1] == T + AHEAD and not (last and uu >= 2 * NC):
                        yield max_row, uu
                if j == QT * (c + 1) - 1:
                    yield read_output, u
                if s == 0:
                    yield w_vo, h
                if more:
                    if s == 1:
                        yield wq_transpose, h + 1
                        if h == 1:
                            yield load, "pe", 2, ("M", ("tq", "head", 2))
                        else:
                            yield load, "o", 1, ("M", ("tq", "head", 1))
                    if s == 2:
                        yield wk_transpose, h + 1
                        yield w_abs, h + 1
                    if s == 4 and h == 1:
                        yield w_pe, 2
                        yield load, "o", 2, ("free", ("pew", "head", 2))
                    for cc, at in enumerate((6, 12, 24, 38)):
                        if s == at:
                            uu = (h + 1) * NC + cc
                            yield q_latent, uu
                            if h == 1:
                                yield q_rope, uu
                                yield load_table, uu + 1 if cc < NC - 1 else 4 * NC, \
                                    (f"d_q{cc}", ("qr", "unit", uu))
                            else:
                                yield q_rope_second, uu
                    if s == 30:
                        yield w_o, h + 1
                        yield wv_transpose, h + 1
                        if not last:
                            yield load, "q", h + 2, ("free", ("wos", "head", h + 1))
                            yield load_kv, h + 2
                if j == QT * (c + 1) - 1:
                    yield denominators, u
                    for t in range(QT):
                        yield head_output, u, t

        parts = {"pre": list(prologue()), "body": list(slots(False)), "last": list(slots(True))}
        whos = ("pe", "act", "dve", "pool", "sp")

        def run(e, who, part, it):
            cn.begin(part, it)
            misc["n"] = {"pre": 0, "body": start["body"], "last": start["last"]}[part]
            prev["v"] = {"pre": [None, None], "body": tail["body"], "last": tail["last"]}[part][:]
            for step, *args in parts[part]:
                step(e, who, *args)

        start, tail = {"body": 0, "last": 0}, {"body": [None, None], "last": [None, None]}
        for part in ("pre", "body", "last"):
            for who in whos:
                run(Silent(), who, part, 0)
            used = misc["n"]
            if part == "pre":
                start["body"] = used % 2
            if part == "body":
                assert (used - start["body"]) % 2 == 0
                start["last"] = start["body"]
                past = [(k[0], k[1], k[2] - PERIOD[k[1]]) + tuple(k[3:]) for k in prev["v"]]
                tail["body"] = tail["last"] = past
        cn.dry = False

        block = ctx.enter_context(nc.Block())
        owner = {"pe": "S G PV M", "act": "exp hi Ph", "dve": "sum max free", "pool": "Pl pool",
                 "sp": " ".join(n for n in names if n.startswith("d_"))}

        def whole(e, who):
            cn.own = idle["sp"] if who == "sp" else None
            for s in owner[who].split():
                if cn.bias(s):
                    e.sem_inc(sems[s], cn.bias(s))
            run(e, who, "pre", 0)
            cn.wait_all(e, "pre")
            with e.Fori(0, NB - 1) as it:
                run(e, who, "body", it)
            run(e, who, "last", NB - 1)

        @block.tensor
        def _(e):
            whole(e, "pe")

        @block.scalar
        def _(e):
            whole(e, "act")

        @block.vector
        def _(e):
            whole(e, "dve")

        @block.gpsimd
        def _(e):
            whole(e, "pool")

        @block.sync
        def _(e):
            whole(e, "sp")
            cn.wait_all(e, "last")


def rope_tables():
    inv = (1.0 / np.float32(10000.0) ** (np.arange(0, ROPE, 2, dtype=np.float32) / np.float32(ROPE)))
    ang = (np.arange(S, dtype=np.float32)[:, None] * inv.astype(np.float32)).astype(np.float32)
    cos, sin = np.cos(ang), np.sin(ang)
    by_row = np.empty((P, 2, S), np.float32)
    by_row[:, 0] = np.tile(cos.T, (4, 1))
    by_row[:, 1] = np.concatenate([-sin.T, -sin.T, sin.T, sin.T])
    by_pos = np.stack([cos, sin], 1).reshape(NT, P, 2, HALF).transpose(1, 0, 2, 3)
    return by_row, np.ascontiguousarray(by_pos)


def kernel(L0_attn_x, L0_attn_wq, L0_attn_wkv_a, L0_attn_wkv_b, L0_attn_wo, L0_attn_kv_norm_scale,
           L0_ffn_factors, L0_ffn_bias):
    import concourse.bacc as bacc
    from concourse.bass_utils import run_bass_kernel_spmd

    rope_t, rope_n = rope_tables()
    arrays = {"x": np.ascontiguousarray(L0_attn_x).reshape(S, E), "wq": L0_attn_wq, "wkv_a": L0_attn_wkv_a,
              "wkv_b": L0_attn_wkv_b, "wo": L0_attn_wo, "kvs": L0_attn_kv_norm_scale,
              "factors": L0_ffn_factors, "bias": L0_ffn_bias, "rope_t": rope_t, "rope_n": rope_n}
    arrays = {n: np.ascontiguousarray(a) for n, a in arrays.items()}
    nc = bacc.Bacc("TRN2", target_bir_lowering=False, num_devices=1,
                   dynamic_dma_scratch_size=1024)
    ins = [nc.dram_tensor(n + "_in", a.shape, F32, kind="ExternalInput").ap() for n, a in arrays.items()]
    out = nc.dram_tensor("layer_out", (S, E), F32, kind="ExternalOutput").ap()
    build(nc, *ins, out)
    r = run_bass_kernel_spmd(nc, [{n + "_in": a for n, a in arrays.items()}], core_ids=[0])
    return r.results[0]["layer_out"].reshape(1, S, E)
```

```python
from contextlib import ExitStack

import numpy as np
import concourse.bass as bass
from concourse import mybir

F32, F32R = mybir.dt.float32, mybir.dt.float32r
F16, BF16 = mybir.dt.float16, mybir.dt.bfloat16
ALU = mybir.AluOpType
ACT = mybir.ActivationFunctionType
AX_X = mybir.AxisListType.X

P = 128
S, E, H = 2048, 512, 16
NOPE, ROPE, VD, LORA, RANK = 128, 64, 128, 128, 8
QH, HALF = NOPE + ROPE, ROPE // 2
CH = 512
NT, NC, KE, QT = S // P, S // CH, E // P, CH // P
SCALE = QH ** -0.5
FIRST = [sum(QT * (i + 1) for i in range(c)) for c in range(NC + 1)]
HT = FIRST[NC]
BT = 2 * HT
LAG, AHEAD = 3, 22
ROW_AT = {5: 2, 20: 3, 28: 4, 32: 5}
NB = H // 2
NEG = -1.0e30
HEADROOM = float(np.log(32.0)) / SCALE
PERIOD = {"tile": BT, "unit": 2 * NC, "head": 2}


def where(tile):
    h, s = divmod(tile, HT)
    c = max(c for c in range(NC) if FIRST[c] <= s)
    return h, c, s - FIRST[c], h * NC + c


class Silent:
    def then_inc(self, *a, **k):
        return self
    matmul = transpose = activation = tensor_copy = tensor_tensor = tensor_scalar = then_inc
    tensor_reduce = tensor_tensor_reduce = scalar_tensor_tensor = reciprocal = memset = then_inc
    bn_stats = bn_aggr = affine_select = dma_start = wait_ge = then_inc


class Counts:

    def __init__(self, sems):
        self.sems = sems
        self.at = {(part, s): {} for part in ("pre", "body", "last") for s in sems}
        self.total = {k: 0 for k in self.at}
        self.dry, self.part, self.it, self.seen, self.own = True, None, 0, {}, None

    def bias(self, s):
        return max(0, self.total["body", s] - self.total["pre", s])

    def begin(self, part, it):
        self.part, self.it, self.seen = part, it, {}

    def inc(self, ins, s, key, n=1):
        if self.dry:
            self.total[self.part, s] += n
            self.at[self.part, s][key] = self.total[self.part, s]
        ins.then_inc(self.sems[s], n)

    def wait(self, eng, s, key):
        if self.dry:
            return
        name, scope, index = key[:3]
        earlier = (name, scope, index + PERIOD[scope]) + tuple(key[3:])
        pre, body = self.total["pre", s], self.total["body", s]
        here = self.at[self.part, s]
        if self.part == "pre":
            if index < 0 and key not in here:
                return
            if key not in here:
                raise KeyError((s, key))
            offset, done = self.bias(s), here[key]
        else:
            offset = self.bias(s) + pre
            if key in here:
                done = here[key]
            elif earlier in self.at["body", s]:
                done = self.at["body", s][earlier] - body
            else:
                raise KeyError((self.part, s, key))
        if self.seen.get(s, -10 ** 9) >= done:
            return
        self.seen[s] = done
        if self.part == "body":
            eng.wait_ge(self.sems[s], self.it * body + (offset + done))
            if self.own:
                eng.sem_inc(self.own, 1)
        else:
            eng.wait_ge(self.sems[s], offset + done + (body * (NB - 1) if self.part == "last" else 0))

    def wait_all(self, eng, part):
        for s in self.sems:
            n = self.bias(s) + self.total["pre", s]
            if part == "last":
                n += body_n(self, s)
            if n:
                eng.wait_ge(self.sems[s], n)


def body_n(counts, s):
    return counts.total["body", s] * (NB - 1) + counts.total["last", s]


def build(nc, x, wq, wkv_a, wkv_b, wo, kvs, factors, bias, rope_t, rope_n, out):
    ctx = ExitStack()
    with ctx:
        def sb(name, shape, dt):
            return ctx.enter_context(nc.sbuf_tensor(name, shape, dt))

        xTh = sb("xTh", [P, KE, S], F32R)
        xTl = sb("xTl", [P, KE, S], F32R)
        kTh = sb("kTh", [P, S], F32R)
        kTl = sb("kTl", [P, S], F32R)
        kR4 = sb("kR4", [P, S], F32R)
        kR5 = sb("kR5", [P, S], F32R)
        vH = sb("vH", [P, NT, LORA], F16)
        vL = sb("vL", [P, NT, LORA], F16)
        acc = sb("acc", [P, NT, E], F32)
        q = sb("q", [P, NC, 4, CH], F32R)
        wAbs = [sb(f"wAbs{i}", [P, KE, LORA], F32R) for i in range(2)]
        wPe = [sb(f"wPe{i}", [P, KE, P], F32R) for i in range(2)]
        wVo = [sb(f"wVo{i}", [P, E], F32R) for i in range(2)]
        wX = [sb(f"wX{i}", [P, KE, P], F32R) for i in range(2)]
        wKT = [sb(f"wKT{i}", [P, LORA], F32R) for i in range(2)]
        wVT = [sb(f"wVT{i}", [P, LORA], F32R) for i in range(2)]
        wst = sb("wst", [P, KE, P], F32)
        wkv = sb("wkv", [P, 2 * P], F32)
        tab = sb("tab", [P, 2, CH], F32)
        ex = sb("ex", [P, 2, CH], F32)
        pH = sb("pH", [P, 4, CH], F16)
        pL = sb("pL", [P, 4, CH], F16)
        esum = sb("esum", [P, 2, CH], F32)
        oH = sb("oH", [P, CH], F32R)
        oL = sb("oL", [P, CH], F32R)
        junk = sb("junk", [P, CH], BF16)
        gmax = sb("gmax", [P, NC, QT * NC], F32)
        rmax = sb("rmax", [P, 2, 2, QT], F32)
        rden = sb("rden", [P, QT], F32)
        ident = sb("ident", [P, P], F32)
        identr = sb("identr", [P, P], F32R)
        upper = sb("upper", [P, P], F32R)
        cmask = sb("cmask", [P, CH], BF16)
        ones = sb("ones", [P, 1], F16)
        eps = sb("eps", [P, 2], F32)
        scl = sb("scl", [P, 1], F32)
        ropen = sb("ropen", [P, NT, 2, HALF], F32)
        stats = sb("stats", [P, NT, 6], F32)
        mv = sb("mv", [P, NT, 2], F32)
        rstd = sb("rstd", [P, 2, NT], F32)
        ssq = sb("ssq", [P, 3, NT], F32)
        ps = ctx.enter_context(nc.psum_tensor("ps", [P, 8, CH], F32))
        SB, GB, OB, MB = 0, 2, 4, 6

        wa_f = pH[:, :, :].rearrange("p a n -> p (a n)").bitcast(F32)[:, 0:KE * QH].rearrange(
            "p (k n) -> p k n", k=KE)
        fsumA = pH[:, :, :].rearrange("p a n -> p (a n)").bitcast(F32).rearrange("p (k n) -> p k n", k=2)
        fsumB = pL[:, :, :].rearrange("p a n -> p (a n)").bitcast(F32).rearrange("p (k n) -> p k n", k=2)
        fsum = [fsumA[:, 0, :], fsumA[:, 1, :], fsumB[:, 0, :], fsumB[:, 1, :]]
        wa = [q[:, i, :, :].rearrange("p a n -> p (a n)")[:, 0:KE * QH].rearrange("p (k n) -> p k n", k=KE)
              for i in range(2)]
        ff = [q[:, 2 + i, :, :] for i in range(2)]
        kt = [tab[:, i, :].rearrange("p (t n) -> p t n", t=2) for i in range(2)]
        biasb = wst[:, :, :].rearrange("p k n -> p (k n)")
        umask = wkv[:, 0:P]
        ktmp = wkv[:, P:2 * P].rearrange("p (a t n) -> p a t n", a=2, t=2)
        sH, sL = [ropen[:, :, :, :].rearrange("p t a n -> p (t a n)").bitcast(F16)[:, i * CH:(i + 1) * CH]
                  for i in range(2)]
        stash = nc.dram_tensor("rope_stash", [NC, 2, P, CH], F32).ap()

        names = ["S", "G", "PV", "M",
                 "exp", "hi", "Ph",
                 "sum", "max", "free",
                 "Pl", "pool",
                 "d_wst", "d_wkv", "d_tab", "d_x", "d_w", "d_c", "d_f0", "d_f1", "d_stash", "d_out"]
        names += [f"d_q{c}" for c in range(NC)]
        sems = {n: ctx.enter_context(nc.semaphore("s_" + n)) for n in names}
        cn = Counts(sems)
        idle = {w: ctx.enter_context(nc.semaphore("idle_" + w)) for w in ("dve", "sp")}
        wait, inc = cn.wait, cn.inc
        misc, bank_of = {"n": 0}, {}

        def f(ap):
            return ap.bitcast(F32)

        def three(e, o, a, b, first=True, last=True):
            e.matmul(o, a[0], b[0], start=first, stop=False)
            e.matmul(o, a[0], b[1], start=False, stop=False)
            return e.matmul(o, a[1], b[0], start=False, stop=last)

        def bank(e, who, key, previous):
            if who == "pe":
                n = misc["n"] % len(previous)
                misc["n"] += 1
                if previous[n] is not None:
                    wait(e, "free", previous[n])
                previous[n] = key
                bank_of[cn.part, key] = [MB, MB + 1, OB, OB + 1][n]
            return ps[:, bank_of[cn.part, key], :]

        prev = {"v": [None, None]}

        def split(e, who, key, src, hi, lo):
            if who == "act":
                wait(e, "M", key)
                inc(e.activation(hi, src, ACT.Copy), "hi", key)
            if who == "dve":
                wait(e, "hi", key)
                inc(e.tensor_tensor(lo, src, f(hi), ALU.subtract), "free", key)

        def constants(e, who):
            k = ("const", "unit", 0)
            if who == "pool":
                e.memset(ones[:, :], 1.0)
                e.memset(eps[:, 0:1], 1e-5)
                e.memset(eps[:, 1:2], 1e-6)
                e.memset(cmask[:, :], 0.0)
                e.memset(umask, 0.0)
                inc(e.memset(ident[:, :], 0.0), "pool", ("zero", "unit", 0))
                wait(e, "pool", ("zero", "unit", 0))
                e.affine_select(out=ident[:, :], in_=ident[:, :], compare_op=ALU.not_equal, fill=1.0,
                                base=0, pattern=[[-1, P]], channel_multiplier=1)
                e.affine_select(out=cmask[:, :], in_=cmask[:, :], compare_op=ALU.is_ge, fill=NEG,
                                base=CH - P, pattern=[[-1, CH]], channel_multiplier=1)
                inc(e.affine_select(out=umask, in_=umask, compare_op=ALU.is_ge, fill=NEG,
                                    base=0, pattern=[[1, P]], channel_multiplier=-1), "pool", k)
            if who == "dve":
                e.memset(f(kR5[HALF * 2:HALF * 3, :]), 1.0)
                wait(e, "pool", k)
                e.tensor_copy(identr[:, :], ident[:, :])
                inc(e.tensor_copy(upper[:, :], umask), "free", k)

        def first_loads(e, who):
            k = ("ld", "unit", 0)
            if who == "sp":
                e.dma_start(acc[:, 0:QT, :], x[0:CH, :].rearrange("(t p) n -> p t n", p=P)) \
                    .then_inc(sems["d_x"], 16)
                cn_add("d_x", ("x", "unit", 0), 16)
                inc(e.dma_start(wa_f, wkv_a.rearrange("(k p) n -> p k n", p=P)), "d_w", k, 16)
                for c in range(1, NC):
                    wait(e, "d_x", ("x", "unit", c - 1))
                    inc(e.dma_start(acc[:, QT * c:QT * c + QT, :],
                                    x[CH * c:CH * c + CH, :].rearrange("(t p) n -> p t n", p=P)),
                        "d_x", ("x", "unit", c), 16)
                    if c == 1:
                        e.dma_start(ropen[:, :, :, :], rope_n).then_inc(sems["d_c"], 16)
                        e.dma_start(scl[:, :], kvs.rearrange("(p a) -> p a", a=1)).then_inc(sems["d_c"], 16)
                        cn_add("d_c", k, 32)
                        inc(e.dma_start(biasb, bias.rearrange("(a n) -> a n", a=1).broadcast_to([P, E])
                                        ), "d_c", k, 16)

        def cn_add(s, key, n):
            if cn.dry:
                cn.total[cn.part, s] += n
                cn.at[cn.part, s][key] = cn.total[cn.part, s]

        def split_wa(e, who):
            k = ("wa", "unit", 0)
            if who == "act":
                wait(e, "d_w", ("ld", "unit", 0))
                inc(e.activation(wa[0], wa_f, ACT.Copy), "hi", k)
            if who == "dve":
                wait(e, "hi", k)
                inc(e.tensor_tensor(wa[1], wa_f, f(wa[0]), ALU.subtract), "free", k)

        def norm_stats(e, who, c):
            ts = slice(QT * c, QT * c + QT)
            if who == "dve":
                wait(e, "d_x", ("x", "unit", c))
                for t in range(QT * c, QT * c + QT):
                    ins = e.bn_stats(stats[:, t, :], acc[:, t, :])
                inc(ins, "free", ("bn", "unit", c))
                wait(e, "free", ("bn", "unit", c))
                for t in range(QT * c, QT * c + QT):
                    ins = e.bn_aggr(mv[:, t, :], stats[:, t, :])
                inc(ins, "free", ("var", "unit", c))
            if who == "act":
                wait(e, "pool", ("const", "unit", 0))
                wait(e, "free", ("var", "unit", c))
                inc(e.activation(rstd[:, 0, ts], mv[:, ts, 1], ACT.Sqrt, bias=eps[:, 0:1]), "hi",
                    ("sd", "unit", c))

        def norm_scale(e, who, c):
            ts = slice(QT * c, QT * c + QT)
            if who == "dve":
                wait(e, "hi", ("sd", "unit", c))
                inc(e.reciprocal(rstd[:, 1, ts], rstd[:, 0, ts]), "free", ("rstd", "unit", c))

        def normalize(e, who, t):
            if who == "dve":
                wait(e, "free", ("rstd", "unit", t // QT))
                if t >= 2:
                    wait(e, "M", ("xt", "unit", t - 2))
                inc(e.tensor_scalar(esum[:, t % 2, :], acc[:, t, :], mv[:, t, 0:1], rstd[:, 1, t:t + 1],
                                    ALU.subtract, ALU.mult), "free", ("xn", "unit", t))

        def transpose_x(e, who, t):
            k = ("xt", "unit", t)
            b = bank(e, who, k, prev["v"])
            xn = esum[:, t % 2, :]
            if who == "pe":
                wait(e, "pool", ("const", "unit", 0))
                wait(e, "free", ("xn", "unit", t))
                for k4 in range(KE):
                    ins = e.transpose(b[:, k4 * P:(k4 + 1) * P], xn[:, k4 * P:(k4 + 1) * P], ident[:, :])
                inc(ins, "M", k)
            if who == "pool":
                wait(e, "d_c", ("ld", "unit", 0))
                wait(e, "free", ("xn", "unit", t))
                inc(e.tensor_tensor(acc[:, t, :], acc[:, t, :], biasb, ALU.add), "pool",
                    ("bias", "unit", t))
            cols = slice(t * P, t * P + P)
            split(e, who, k, b.rearrange("p (k n) -> p k n", k=KE), xTh[:, :, cols], xTl[:, :, cols])

        def latent(e, who, p2):
            k = ("kva", "unit", p2)
            b = bank(e, who, k, prev["v"])[:, 0:2 * QH].rearrange("p (t n) -> p t n", t=2)
            ts = slice(2 * p2, 2 * p2 + 2)
            cos, sin = ropen[:, ts, 0, :], ropen[:, ts, 1, :]
            lo, hi = b[:, :, LORA:LORA + HALF], b[:, :, LORA + HALF:QH]
            kk = kt[p2 % 2]
            r1, r2 = kk[:, :, LORA:LORA + HALF], kk[:, :, LORA + HALF:LORA + ROPE]
            if who == "pe":
                wait(e, "free", ("wa", "unit", 0))
                wait(e, "free", ("xt", "unit", 2 * p2 + 1))
                for i in range(2):
                    cols = slice((2 * p2 + i) * P, (2 * p2 + i + 1) * P)
                    for k4 in range(KE):
                        ins = three(e, b[:, i, :], [xTh[:, k4, cols], xTl[:, k4, cols]],
                                    [wa[0][:, k4, :], wa[1][:, k4, :]], k4 == 0, k4 == KE - 1)
                inc(ins, "M", k)
            if who == "act":
                wait(e, "M", k)
                for i in range(2):
                    if 2 * p2 + i:
                        wait(e, "hi", ("sq", "unit", 2 * p2 + i - 1))
                    inc(e.activation(junk[:, 0:LORA], b[:, i, 0:LORA], ACT.Square,
                                     accum_out=ssq[:, 0, 2 * p2 + i:2 * p2 + i + 1]), "hi",
                        ("sq", "unit", 2 * p2 + i))
                wait(e, "hi", ("sq", "unit", 2 * p2 + 1))
                inc(e.activation(ssq[:, 1, ts], ssq[:, 0, ts], ACT.Sqrt, bias=eps[:, 1:2],
                                 scale=1.0 / LORA), "hi", ("rms", "unit", p2))
            if who == "dve":
                wait(e, "d_c", ("ld", "unit", 0))
                wait(e, "hi", ("rms", "unit", p2))
                inc(e.reciprocal(ssq[:, 2, ts], ssq[:, 1, ts]), "free", ("rr", "unit", p2))
                if p2 >= 2:
                    wait(e, "M", ("kT", "unit", p2 - 2))
                    wait(e, "free", ("vL", "unit", p2 - 2))
                wait(e, "free", ("rr", "unit", p2))
                for i in range(2):
                    e.tensor_scalar(kk[:, i, 0:LORA], b[:, i, 0:LORA], ssq[:, 2, 2 * p2 + i:2 * p2 + i + 1],
                                    None, ALU.mult)
                e.tensor_tensor(r1, lo, cos, ALU.mult)
                e.tensor_tensor(ktmp[:, 0, :, :], hi, sin, ALU.mult)
                e.tensor_tensor(r2, hi, cos, ALU.mult)
                inc(e.tensor_tensor(ktmp[:, 1, :, :], lo, sin, ALU.mult), "free", k)
                wait(e, "free", k)
                e.tensor_tensor(r1, r1, ktmp[:, 0, :, :], ALU.subtract)
                inc(e.tensor_tensor(r2, r2, ktmp[:, 1, :, :], ALU.add), "free", ("rope", "unit", p2))
                wait(e, "free", ("rope", "unit", p2))
                inc(e.tensor_copy(kk[:, :, LORA + ROPE:2 * P], kk[:, :, LORA:LORA + ROPE]), "free",
                    ("kk", "unit", p2))

        def value_parts(e, who, p2):
            kk, ts = kt[p2 % 2], slice(2 * p2, 2 * p2 + 2)
            if who == "act":
                wait(e, "free", ("kk", "unit", p2))
                inc(e.activation(vH[:, ts, :], kk[:, :, 0:LORA], ACT.Copy), "hi", ("vH", "unit", p2))
            if who == "dve":
                wait(e, "hi", ("vH", "unit", p2))
                inc(e.tensor_tensor(vL[:, ts, :], kk[:, :, 0:LORA], vH[:, ts, :], ALU.subtract), "free",
                    ("vL", "unit", p2))

        def keys(e, who, p2):
            k = ("kT", "unit", p2)
            b = bank(e, who, k, prev["v"])
            kk = kt[p2 % 2]
            cols = slice(2 * p2 * P, (2 * p2 + 2) * P)
            if who == "pe":
                wait(e, "free", ("kk", "unit", p2))
                for i in range(2):
                    e.transpose(b[:, i * P:(i + 1) * P], kk[:, i, 0:P], ident[:, :])
                    ins = e.transpose(b[:, (2 + i) * P:(3 + i) * P], kk[:, i, P:2 * P], ident[:, :])
                inc(ins, "M", k)
            if who == "act":
                wait(e, "M", k)
                e.activation(kTh[:, cols], b[:, 0:2 * P], ACT.Copy)
                inc(e.activation(kR4[:, cols], b[:, 2 * P:4 * P], ACT.Copy), "hi", k)
            if who == "dve":
                wait(e, "hi", k)
                e.tensor_tensor(kTl[:, cols], b[:, 0:2 * P], f(kTh[:, cols]), ALU.subtract)
                inc(e.tensor_tensor(kR5[0:ROPE, cols], b[0:ROPE, 2 * P:4 * P], f(kR4[0:ROPE, cols]),
                                    ALU.subtract), "free", k)

        def factor(e, who, i):
            r, k4 = divmod(i, KE)
            k = ("fac", "unit", i)
            src = factors[r, k4 * P:(k4 + 1) * P, :]
            if r == 0:
                if who == "sp":
                    wait(e, "free", ("wa", "unit", 0))
                    ins = e.dma_start(fsum[k4], src)
                    ins.then_inc(sems["d_w"], 16)
                    cn_add("d_w", k, 16)
                return
            if who == "sp":
                if i >= KE + 2:
                    wait(e, "pool", ("fac", "unit", i - 2))
                inc(e.dma_start(ex[:, i % 2, :], src), f"d_f{i % 2}", k, 16)
            if who == "pool":
                wait(e, "d_w", ("fac", "unit", KE - 1))
                wait(e, f"d_f{i % 2}", k)
                if r > 1:
                    wait(e, "pool", ("fac", "unit", i - KE))
                inc(e.tensor_tensor(fsum[k4], fsum[k4], ex[:, i % 2, :], ALU.add), "pool", k)

        def split_ff(e, who):
            for k4 in range(KE):
                k = ("ff", "unit", k4)
                if who == "act":
                    wait(e, "pool", ("fac", "unit", RANK * KE - KE + k4))
                    inc(e.activation(ff[0][:, k4, :], fsum[k4], ACT.Copy), "hi", k)
                if who == "dve":
                    wait(e, "hi", k)
                    inc(e.tensor_tensor(ff[1][:, k4, :], fsum[k4], f(ff[0][:, k4, :]), ALU.subtract),
                        "free", k)

        def ffn(e, who, t):
            k = ("ffn", "unit", t)
            b = bank(e, who, k, prev["v"])
            cols = slice(t * P, t * P + P)
            if who == "pe":
                wait(e, "free", ("xt", "unit", t))
                wait(e, "free", ("ff", "unit", KE - 1))
                for k4 in range(KE):
                    ins = three(e, b, [xTh[:, k4, cols], xTl[:, k4, cols]],
                                [ff[0][:, k4, :], ff[1][:, k4, :]], k4 == 0, k4 == KE - 1)
                inc(ins, "M", k)
            if who == "dve":
                wait(e, "M", k)
                wait(e, "pool", ("bias", "unit", t))
                inc(e.scalar_tensor_tensor(out=acc[:, t, :], in0=b, scalar=float(RANK) ** -0.5,
                                           in1=acc[:, t, :], op0=ALU.mult, op1=ALU.add), "free", k)

        def head0():
            return cn.it * 2

        def load(e, who, kind, h, after):
            if who != "sp":
                return
            wait(e, after[0], after[1])
            k = ("w" + kind, "head", h)
            wqv = wq.rearrange("(k p) n -> p k n", p=P)
            hh = head0() + h
            if kind == "q":
                inc(e.dma_start(wst[:, :, :], wqv[:, :, bass.ds(hh * QH, NOPE)]), "d_wst", k, 16)
            if kind == "o":
                inc(e.dma_start(wst[:, :, :], wo[bass.ds(hh * VD, VD), :].rearrange(
                    "p (k n) -> p k n", k=KE)), "d_wst", k, 16)
            if kind == "pe":
                for half in range(2):
                    for b in range(2):
                        at = (2 * half + b) * HALF
                        ins = e.dma_start(wst[:, :, at:at + HALF],
                                          wqv[:, :, bass.ds(hh * QH + b * QH + NOPE + half * HALF, HALF)])
                        inc(ins, "d_wst", k, 16)

        def load_kv(e, who, h, first=False):
            if who == "sp":
                if first:
                    wait(e, "free", ("rope", "unit", NT // 2 - 1))
                else:
                    wait(e, "M", ("wvt", "head", h - 1))
                inc(e.dma_start(wkv[:, :], wkv_b[:, bass.ds((head0() + h) * 2 * P, 2 * P)]), "d_wkv",
                    ("wkv", "head", h), 16)

        def scale_kv(e, who, h):
            if who == "dve":
                if cn.part == "pre":
                    wait(e, "d_c", ("ld", "unit", 0))
                wait(e, "d_wkv", ("wkv", "head", h))
                inc(e.tensor_scalar(wkv[:, :], wkv[:, :], scl[:, 0:1], None, ALU.mult), "free",
                    ("kvs", "head", h))

        def wq_transpose(e, who, h):
            k = ("tq", "head", h)
            b = bank(e, who, k, prev["v"])
            if who == "pe":
                wait(e, "d_wst", ("wq", "head", h))
                for k4 in range(KE):
                    ins = e.transpose(b[:, k4 * P:(k4 + 1) * P], wst[:, k4, :], ident[:, :])
                inc(ins, "M", k)
            if who == "act" and not (cn.part == "pre"):
                wait(e, "M", ("wvo", "head", h - 1))
            split(e, who, k, b.rearrange("p (k n) -> p k n", k=KE), wX[0][:, :, :], wX[1][:, :, :])

        def wk_transpose(e, who, h):
            k = ("tk", "head", h)
            b = bank(e, who, k, prev["v"])[:, 0:P]
            if who == "pe":
                wait(e, "free", ("kvs", "head", h))
                inc(e.transpose(b, wkv[:, 0:P], ident[:, :]), "M", k)
            split(e, who, k, b, wKT[0][:, :], wKT[1][:, :])

        def w_abs(e, who, h):
            k = ("wabs", "head", h)
            b = bank(e, who, k, prev["v"])
            if who == "pe":
                wait(e, "free", ("tq", "head", h))
                wait(e, "free", ("tk", "head", h))
                for k4 in range(KE):
                    ins = three(e, b[:, k4 * P:(k4 + 1) * P], [w[:, k4, :] for w in wX],
                                [w[:, :] for w in wKT])
                inc(ins, "M", k)
            split(e, who, k, b.rearrange("p (k n) -> p k n", k=KE), wAbs[0][:, :, :], wAbs[1][:, :, :])

        def w_pe(e, who, h):
            k = ("pew", "head", h)
            if who == "act":
                wait(e, "d_wst", ("wpe", "head", h))
                if cn.part != "pre":
                    wait(e, "M", ("pe", "unit", (h - 2) * NC + NC - 1))
                inc(e.activation(wPe[0][:, :, :], wst[:, :, :], ACT.Copy), "hi", k)
            if who == "dve":
                wait(e, "hi", k)
                inc(e.tensor_tensor(wPe[1][:, :, :], wst[:, :, :], f(wPe[0][:, :, :]), ALU.subtract),
                    "free", k)

        def wv_transpose(e, who, h):
            k = ("wvt", "head", h)
            b = bank(e, who, k, prev["v"])[:, 0:P]
            if who == "pe":
                wait(e, "free", ("kvs", "head", h))
                inc(e.transpose(b, wkv[:, P:2 * P], ident[:, :]), "M", k)
            split(e, who, k, b, wVT[0][:, :], wVT[1][:, :])

        def w_o(e, who, h):
            k = ("wos", "head", h)
            if who == "act":
                wait(e, "d_wst", ("wo", "head", h))
                wait(e, "M", ("wabs", "head", h) if cn.part == "pre" else ("wabs", "head", h))
                inc(e.activation(wX[0][:, :, :], wst[:, :, :], ACT.Copy), "hi", k)
            if who == "dve":
                wait(e, "hi", k)
                inc(e.tensor_tensor(wX[1][:, :, :], wst[:, :, :], f(wX[0][:, :, :]), ALU.subtract),
                    "free", k)

        def w_vo(e, who, h):
            k = ("wvo", "head", h)
            b = bank(e, who, k, prev["v"])
            if who == "pe":
                wait(e, "free", ("wos", "head", h))
                wait(e, "free", ("wvt", "head", h))
                ins = three(e, b, [w[:, :] for w in wVT], [w[:, :, :].rearrange("p k n -> p (k n)") for w in wX])
                inc(ins, "M", k)
            split(e, who, k, b, wVo[0][:, :], wVo[1][:, :])

        def q_latent(e, who, u):
            h, c = divmod(u, NC)
            k = ("q", "unit", u)
            b = bank(e, who, k, prev["v"])
            cols = slice(c * CH, c * CH + CH)
            if who == "pe":
                wait(e, "free", ("wabs", "head", h))
                for k4 in range(KE):
                    ins = three(e, b, [w[:, k4, :] for w in wAbs], [xTh[:, k4, cols], xTl[:, k4, cols]],
                                k4 == 0, k4 == KE - 1)
                inc(ins, "M", k)
            if who == "act" and cn.part != "pre":
                wait(e, "S", last_tile(u - NC))
            split(e, who, k, b, q[:, c, 0, :], q[:, c, 1, :])

        def last_tile(u):
            h, c = divmod(u, NC)
            return ("s", "tile", h * HT + FIRST[c + 1] - 1)

        def load_table(e, who, u, *after):
            if who == "sp":
                for a in after:
                    wait(e, *a)
                c = u % NC
                inc(e.dma_start(tab[:, :, :], rope_t[:, :, c * CH:(c + 1) * CH]), "d_tab",
                    ("tab", "unit", u), 16)

        def q_rope(e, who, u):
            h, c = divmod(u, NC)
            k = ("pe", "unit", u)
            b = bank(e, who, k, prev["v"])
            cols = slice(c * CH, c * CH + CH)
            cos, sin = tab[:, 0, :], tab[:, 1, :]
            if who == "pe":
                wait(e, "free", ("pew", "head", h))
                for k4 in range(KE):
                    ins = three(e, b, [w[:, k4, :] for w in wPe], [xTh[:, k4, cols], xTl[:, k4, cols]],
                                k4 == 0, k4 == KE - 1)
                inc(ins, "M", k)
            if who == "dve":
                wait(e, "d_tab", ("tab", "unit", u))
                wait(e, "M", k)
                e.tensor_tensor(cos, b, cos, ALU.mult)
                e.tensor_tensor(sin[0:ROPE, :], b[ROPE:P, :], sin[0:ROPE, :], ALU.mult)
                inc(e.tensor_tensor(sin[ROPE:P, :], b[0:ROPE, :], sin[ROPE:P, :], ALU.mult), "free", k)
            if who == "pool":
                wait(e, "free", k)
                inc(e.tensor_tensor(cos, cos, sin, ALU.add), "pool", ("ro", "unit", u))

        def rope_parts(e, who, u):
            h, c = divmod(u, NC)
            k = ("pe", "unit", u)
            cos, sin = tab[:, 0, :], tab[:, 1, :]
            if who == "pool":
                wait(e, "hi", k)
                inc(e.tensor_tensor(cos, cos, sin, ALU.subtract), "pool", k)
            if who == "act":
                wait(e, "pool", ("ro", "unit", u))
                inc(e.activation(sin.bitcast(F32R), cos, ACT.Copy), "hi", k)
            if who == "sp":
                wait(e, "pool", k)
                if cn.part != "pre":
                    wait(e, f"d_q{c}", ("qr", "unit", u - NC))
                inc(e.dma_start(stash[c].rearrange("a p n -> p a n"), tab[:, :, :]), "d_stash", k, 16)
                if cn.part != "pre":
                    wait(e, "S", last_tile(u - NC))
                fill(e, u, [tab[:, i, :] for i in range(2)], 0)

        def fill(e, u, lohi, b):
            c = u % NC
            lo, hi = lohi
            for half in range(2):
                src = slice((2 * half + b) * HALF, (2 * half + b + 1) * HALF)
                dst = half * HALF
                e.dma_start(f(q[dst:dst + HALF, c, 2, :]), hi[src, :]).then_inc(sems[f"d_q{c}"], 16)
                e.dma_start(f(q[dst:dst + HALF, c, 3, :]), hi[src, :]).then_inc(sems[f"d_q{c}"], 16)
                cn_add(f"d_q{c}", None, 32)
                inc(e.dma_start(f(q[ROPE + dst:ROPE + dst + HALF, c, 2, :]), lo[src, :]), f"d_q{c}",
                    ("qr", "unit", u), 16)

        def q_rope_second(e, who, u):
            if who == "sp":
                wait(e, "d_stash", ("pe", "unit", u - NC))
                wait(e, "S", last_tile(u - NC))
                fill(e, u, [stash[u % NC, i] for i in range(2)], 1)

        def group(e, who, g):
            h, c, j, u = where(g)
            t, kg = divmod(j, c + 1)
            k = ("g", "tile", g)
            n = CH if kg < c else (t + 1) * P
            b = ps[:, GB + g % 2, 0:n]
            qs, ks = slice(t * P, t * P + P), slice(kg * CH, kg * CH + n)
            m = gmax[:, u % NC, t * NC + kg:t * NC + kg + 1]
            if who == "pe":
                wait(e, "max", ("g", "tile", g - 2))
                if j == 0:
                    wait(e, "free", ("q", "unit", u))
                e.matmul(b, q[:, c, 0, qs], kTh[:, ks], start=True, stop=False)
                if j == 0:
                    wait(e, f"d_q{c}", ("qr", "unit", u))
                inc(e.matmul(b, q[0:ROPE, c, 2, qs], kR4[0:ROPE, ks], start=False, stop=True), "G", k)
            if who == "dve":
                wait(e, "max", ("g", "tile", g - 1))
                wait(e, "G", k)
                if kg < c:
                    inc(e.tensor_reduce(m, b, AX_X, ALU.max), "max", k)
                else:
                    if cn.part == "body" and not cn.dry:
                        e.sem_inc(idle["dve"], 1)
                    inc(e.tensor_tensor_reduce(out=junk[:, 0:n], in0=b, in1=cmask[:, CH - n:CH], scale=1.0,
                                               scalar=NEG, op0=ALU.add, op1=ALU.max, accum_out=m), "max", k)

        def max_column(e, who, u):
            h, c = divmod(u, NC)
            gm = gmax[:, u % NC, :].rearrange("p (t g) -> p t g", t=QT)[:, :, 0:c + 1]
            if who == "dve":
                wait(e, "max", ("g", "tile", h * HT + FIRST[c + 1] - 1))
                inc(e.tensor_reduce(rmax[:, u % 2, 0, :], gm, AX_X, ALU.max), "free", ("rm", "unit", u))
                wait(e, "free", ("rm", "unit", u))
                inc(e.tensor_scalar(rmax[:, u % 2, 1, :], rmax[:, u % 2, 0, :], -1.0, HEADROOM, ALU.mult, ALU.add),
                    "free", ("nm", "unit", u))

        def max_row(e, who, u):
            h, c = divmod(u, NC)
            k = ("mT", "unit", u)
            b = bank(e, who, k, prev["v"])[0:QT, 0:P]
            if who == "dve":
                wait(e, "M", k)
                qq = q[ROPE:ROPE + QT, c, 3, :].rearrange("p (t n) -> p t n", t=QT)
                inc(e.tensor_tensor(qq, b.unsqueeze(1).broadcast_to([QT, QT, P]),
                                    ident[0:QT, 0:QT].unsqueeze(2).broadcast_to([QT, QT, P]), ALU.mult),
                    "free", k)
            if who == "pe":
                wait(e, "free", ("nm", "unit", u))
                inc(e.transpose(b, rmax[:, u % 2, 1, :], ident[:, :]), "M", k)

        def scores(e, who, T):
            h, c, j, u = where(T)
            k = ("s", "tile", T)
            n0 = max(0, j - QT * c) * P
            b = ps[:, SB + T % 2, n0:CH]
            ks = slice(j * P, j * P + P)
            x2, x4 = T % 2, T % 4
            if who == "pe":
                wait(e, "exp", ("s", "tile", T - 2))
                if j == 0:
                    wait(e, "free", ("mT", "unit", u))
                three(e, b, [kTh[:, ks], kTl[:, ks]], [q[:, c, 0, n0:], q[:, c, 1, n0:]], True, False)
                if j >= QT * c:
                    e.matmul(ps[:, SB + T % 2, n0:n0 + P], identr[:, :], upper[:, :], start=False, stop=False)
                e.matmul(b, kR4[:, ks], q[:, c, 2, n0:], start=False, stop=False)
                inc(e.matmul(b, kR5[0:ROPE + QT, ks], q[0:ROPE + QT, c, 3, n0:], start=False, stop=True),
                    "S", k)
            if who == "act":
                wait(e, "sum", ("s", "tile", T - 2))
                wait(e, "Pl", ("s", "tile", T - 2))
                wait(e, "S", k)
                inc(e.activation(ex[:, x2, n0:], b, ACT.Exp, scale=SCALE), "exp", k)
                wait(e, "PV", ("s", "tile", T - 4))
                wait(e, "exp", k)
                inc(e.activation(pH[:, x4, n0:], ex[:, x2, n0:], ACT.Copy), "Ph", k)
            if who == "pool":
                wait(e, "Ph", k)
                inc(e.tensor_tensor(pL[:, x4, n0:], ex[:, x2, n0:], pH[:, x4, n0:], ALU.subtract), "Pl", k)

        def row_sum(e, who, T):
            h, c, j, u = where(T)
            n0 = max(0, j - QT * c) * P
            if who == "dve":
                k = ("s", "tile", T)
                wait(e, "exp", k)
                es = esum[:, u % 2, n0:]
                if j == 0:
                    wait(e, "pool", ("es", "unit", u - 2))
                    inc(e.tensor_copy(es, ex[:, T % 2, n0:]), "sum", k)
                else:
                    wait(e, "sum", ("s", "tile", T - 1))
                    inc(e.tensor_tensor(es, es, ex[:, T % 2, n0:], ALU.add), "sum", k)

        def values(e, who, T):
            h, c, j, u = where(T)
            n0 = max(0, j - QT * c) * P
            if who == "pe":
                k = ("s", "tile", T)
                if j == 0:
                    wait(e, "free", ("o", "unit", u - 2))
                if T == 0 and cn.part == "pre":
                    for k0 in prev["v"][2:]:
                        wait(e, "free", k0)
                wait(e, "Pl", k)
                inc(three(e, ps[:, OB + u % 2, n0:], [vH[:, j, :], vL[:, j, :]],
                          [pH[:, T % 4, n0:], pL[:, T % 4, n0:]], j == 0, j == QT * (c + 1) - 1), "PV", k)

        def split_sums(e, who, u):
            h, c = divmod(u, NC)
            k = ("es", "unit", u)
            if who == "act":
                wait(e, "sum", ("s", "tile", h * HT + FIRST[c + 1] - 1))
                wait(e, "M", ("den", "unit", u - 1))
                inc(e.activation(sH, esum[:, u % 2, :], ACT.Copy), "hi", k)
            if who == "pool":
                wait(e, "hi", k)
                inc(e.tensor_tensor(sL, esum[:, u % 2, :], sH, ALU.subtract), "pool", k)

        def denominators(e, who, u):
            k = ("den", "unit", u)
            b = bank(e, who, k, prev["v"])[:, 0:QT]
            if who == "pe":
                wait(e, "pool", ("es", "unit", u))
                for t in range(QT):
                    qs = slice(t * P, (t + 1) * P)
                    e.matmul(b[:, t:t + 1], sH[:, qs], ones[:, :], start=True, stop=False)
                    ins = e.matmul(b[:, t:t + 1], sL[:, qs], ones[:, :], start=False, stop=True)
                inc(ins, "M", k)
            if who == "dve":
                wait(e, "M", k)
                inc(e.reciprocal(rden[:, :], b), "free", k)

        def read_output(e, who, u):
            h, c = divmod(u, NC)
            k = ("o", "unit", u)
            b = ps[:, OB + u % 2, :]
            if who == "act":
                wait(e, "PV", ("s", "tile", h * HT + FIRST[c + 1] - 1))
                wait(e, "M", ("out", "unit", u - 1, QT - 1))
                inc(e.activation(oH[:, :], b, ACT.Copy), "hi", k)
            if who == "dve":
                wait(e, "hi", k)
                inc(e.tensor_tensor(oL[:, :], b, f(oH[:, :]), ALU.subtract), "free", k)

        def head_output(e, who, u, t):
            h, c = divmod(u, NC)
            k = ("out", "unit", u, t)
            b = bank(e, who, k, prev["v"])
            if who == "pe":
                wait(e, "free", ("o", "unit", u))
                wait(e, "free", ("wvo", "head", h))
                inc(three(e, b, [oH[:, t * P:(t + 1) * P], oL[:, t * P:(t + 1) * P]], [w[:, :] for w in wVo]),
                    "M", k)
            a = acc[:, QT * c + t, :]
            if who == "dve":
                wait(e, "M", k)
                wait(e, "free", ("den", "unit", u))
                inc(e.scalar_tensor_tensor(out=a, in0=b, scalar=rden[:, t:t + 1], in1=a, op0=ALU.mult,
                                           op1=ALU.add), "free", k)
            if who == "sp" and cn.part == "last" and h == 1:
                wait(e, "free", k)
                inc(e.dma_start(out[(QT * c + t) * P:(QT * c + t + 1) * P, :], a), "d_out", k, 16)

        def prologue():
            yield constants,
            yield first_loads,
            yield split_wa,
            yield norm_stats, 0
            yield norm_scale, 0
            yield normalize, 0
            facs = iter(range(RANK * KE))
            for t in range(NT + 4):
                if t < NT:
                    if t % QT == 1 and t // QT + 1 < NC:
                        yield norm_stats, t // QT + 1
                    if t % QT == 3 and t // QT + 1 < NC:
                        yield norm_scale, t // QT + 1
                    if t + 1 < NT:
                        yield normalize, t + 1
                if t % 2 == 0 and 0 <= t // 2 - 2 < NT // 2:
                    yield "dve", latent, t // 2 - 2
                if t < NT:
                    yield transpose_x, t
                if t % 2 == 0 and 0 <= t // 2 - 2 < NT // 2:
                    yield value_parts, t // 2 - 2
                if t < NT:
                    for _, i in zip(range(3), facs):
                        yield factor, i
                if t % 2 == 1:
                    if 0 <= t // 2 - 1 < NT // 2:
                        yield "pe act", latent, t // 2 - 1
                    if 0 <= t // 2 - 2 < NT // 2:
                        yield keys, t // 2 - 2
            yield load, "q", 0, ("pool", ("bias", "unit", NT - 1))
            yield load_kv, 0, True
            yield load_table, 0, ("M", ("kT", "unit", NT // 2 - 1)), ("free", ("vL", "unit", NT // 2 - 1))
            yield split_ff,
            yield scale_kv, 0
            yield wq_transpose, 0
            yield load, "pe", 0, ("M", ("tq", "head", 0))
            yield wk_transpose, 0
            yield ffn, 0
            yield w_abs, 0
            yield ffn, 1
            yield w_pe, 0
            yield load, "o", 0, ("free", ("pew", "head", 0))
            for c in range(NC):
                yield q_rope, c
                yield rope_parts, c
                yield load_table, c + 1 if c < NC - 1 else 2 * NC, (f"d_q{c}", ("qr", "unit", c))
                yield q_latent, c
                if c == 0:
                    for t in range(2, 9):
                        yield ffn, t
                    yield w_o, 0
                if c == 1:
                    for t in range(9, NT):
                        yield ffn, t
                    yield wv_transpose, 0
                    yield load, "q", 1, ("free", ("wos", "head", 0))
                    yield load_kv, 1
                if c == 2:
                    for g in range(FIRST[2]):
                        yield group, g
                    for u in range(2):
                        yield max_column, u
            for g in range(FIRST[2], AHEAD):
                yield group, g
                if g == FIRST[2] + 1:
                    for u in range(2):
                        yield max_row, u
            for T in range(LAG):
                yield scores, T
                if T:
                    yield row_sum, T - 1
            yield from slots(0, FIRST[1])

        def slots(first, end, last=False):
            late = []

            def task(step, *args):
                if sum(isinstance(x[0], str) for x in late) >= 2:
                    yield from late
                    late.clear()
                late.append(("act dve pool sp", step, *args))
                yield ("pe", step, *args)

            for T in range(first, end):
                h, c, j, u = where(T)
                s = T % HT
                more = not last or h == 0
                yield from late
                late.clear()
                yield values, T
                if not last or T + LAG < BT:
                    yield scores, T + LAG
                if not last or T + AHEAD < BT:
                    yield group, T + AHEAD
                if not last or T + LAG - 1 < BT:
                    yield row_sum, T + LAG - 1
                for uu in range(2, 3 * NC):
                    hh, cc = divmod(uu, NC)
                    if not (last and uu >= 2 * NC):
                        if hh * HT + FIRST[cc + 1] == T + AHEAD:
                            yield max_column, uu
                if s in ROW_AT and not (last and h * NC + ROW_AT[s] >= 2 * NC):
                    yield from task(max_row, h * NC + ROW_AT[s])
                if u and j == 1:
                    yield from task(denominators, u - 1)
                if u and j in (2, 3):
                    for t in range(2 * j - 4, 2 * j - 2):
                        yield from task(head_output, u - 1, t)
                if j == QT * (c + 1) - 1:
                    yield split_sums, u
                    yield read_output, u
                if s == 4:
                    yield from task(w_vo, h)
                if more:
                    if s == 4:
                        yield scale_kv, h + 1
                        yield from task(wq_transpose, h + 1)
                        if h == 1:
                            yield load, "pe", 2, ("M", ("tq", "head", 2))
                        else:
                            yield load, "o", 1, ("M", ("tq", "head", 1))
                    if s == 8:
                        yield from task(wk_transpose, h + 1)
                    if s == 10:
                        yield from task(w_abs, h + 1)
                    if s == 8 and h == 1:
                        yield w_pe, 2
                        yield load, "o", 2, ("free", ("pew", "head", 2))
                    for cc, (at, at_rope) in enumerate(((12, 10), (18, 17), (23, 22), (37, 34))):
                        uu = (h + 1) * NC + cc
                        if s == at_rope and h == 1:
                            yield from task(q_rope, uu)
                        if s == at_rope + 2 and h == 1:
                            yield rope_parts, uu
                            yield load_table, uu + 1 if cc < NC - 1 else 4 * NC, (f"d_q{cc}", ("qr", "unit", uu))
                        if s == at:
                            yield from task(q_latent, uu)
                            if h == 0:
                                yield q_rope_second, uu
                    if s == 30:
                        yield w_o, h + 1
                        yield from task(wv_transpose, h + 1)
                        if not last:
                            yield load, "q", h + 2, ("free", ("wos", "head", h + 1))
                            yield load_kv, h + 2
            yield from late
            if last:
                yield denominators, u
                for t in range(QT):
                    yield head_output, u, t

        whos = ("pe", "act", "dve", "pool", "sp")
        parts = {"pre": prologue(), "body": slots(FIRST[1], BT + FIRST[1]),
                 "last": slots(FIRST[1], BT, True)}
        parts = {part: [(x[0].split(), *x[1:]) if isinstance(x[0], str) else (whos, *x) for x in steps]
                 for part, steps in parts.items()}

        def run(e, who, part, it):
            cn.begin(part, it)
            misc["n"] = {"pre": 0, "body": start["body"], "last": start["last"]}[part]
            prev["v"] = {"pre": [None] * 4, "body": tail["body"], "last": tail["last"]}[part][:]
            for whom, step, *args in parts[part]:
                if who in whom:
                    step(e, who, *args)

        start, tail = {"body": 0, "last": 0}, {"body": [None, None], "last": [None, None]}
        for part in ("pre", "body", "last"):
            for who in whos:
                run(Silent(), who, part, 0)
                if who == "pe":
                    used, users = misc["n"], prev["v"]
            if part == "pre":
                start["body"] = 0
            if part == "body":
                assert (used - start["body"]) % 2 == 0
                start["last"] = start["body"]
                past = [(k[0], k[1], k[2] - PERIOD[k[1]]) + tuple(k[3:]) for k in users]
                tail["body"] = tail["last"] = past
        cn.dry = False

        block = ctx.enter_context(nc.Block())
        owner = {"pe": "S G PV M", "act": "exp hi Ph", "dve": "sum max free", "pool": "Pl pool",
                 "sp": " ".join(n for n in names if n.startswith("d_"))}

        def whole(e, who):
            cn.own = idle["sp"] if who == "sp" else None
            for s in owner[who].split():
                if cn.bias(s):
                    e.sem_inc(sems[s], cn.bias(s))
            run(e, who, "pre", 0)
            cn.wait_all(e, "pre")
            with e.Fori(0, NB - 1) as it:
                run(e, who, "body", it)
            run(e, who, "last", NB - 1)

        @block.tensor
        def _(e):
            whole(e, "pe")

        @block.scalar
        def _(e):
            whole(e, "act")

        @block.vector
        def _(e):
            whole(e, "dve")

        @block.gpsimd
        def _(e):
            whole(e, "pool")

        @block.sync
        def _(e):
            whole(e, "sp")
            cn.wait_all(e, "last")


def rope_tables():
    inv = (1.0 / np.float32(10000.0) ** (np.arange(0, ROPE, 2, dtype=np.float32) / np.float32(ROPE)))
    ang = (np.arange(S, dtype=np.float32)[:, None] * inv.astype(np.float32)).astype(np.float32)
    cos, sin = np.cos(ang), np.sin(ang)
    by_row = np.empty((P, 2, S), np.float32)
    by_row[:, 0] = np.tile(cos.T, (4, 1))
    by_row[:, 1] = np.concatenate([-sin.T, -sin.T, sin.T, sin.T])
    by_pos = np.stack([cos, sin], 1).reshape(NT, P, 2, HALF).transpose(1, 0, 2, 3)
    return by_row, np.ascontiguousarray(by_pos)


def kernel(L0_attn_x, L0_attn_wq, L0_attn_wkv_a, L0_attn_wkv_b, L0_attn_wo, L0_attn_kv_norm_scale,
           L0_ffn_factors, L0_ffn_bias):
    import concourse.bacc as bacc
    from concourse.bass_utils import run_bass_kernel_spmd

    rope_t, rope_n = rope_tables()
    arrays = {"x": np.ascontiguousarray(L0_attn_x).reshape(S, E), "wq": L0_attn_wq, "wkv_a": L0_attn_wkv_a,
              "wkv_b": L0_attn_wkv_b, "wo": L0_attn_wo, "kvs": L0_attn_kv_norm_scale,
              "factors": L0_ffn_factors, "bias": L0_ffn_bias, "rope_t": rope_t, "rope_n": rope_n}
    arrays = {n: np.ascontiguousarray(a) for n, a in arrays.items()}
    nc = bacc.Bacc("TRN2", target_bir_lowering=False, num_devices=1,
                   dynamic_dma_scratch_size=1024)
    ins = [nc.dram_tensor(n + "_in", a.shape, F32, kind="ExternalInput").ap() for n, a in arrays.items()]
    out = nc.dram_tensor("layer_out", (S, E), F32, kind="ExternalOutput").ap()
    build(nc, *ins, out)
    r = run_bass_kernel_spmd(nc, [{n + "_in": a for n, a in arrays.items()}], core_ids=[0])
    return r.results[0]["layer_out"].reshape(1, S, E)
```

```python
from contextlib import ExitStack

import numpy as np
import concourse.bass as bass
from concourse import mybir

F32, F32R = mybir.dt.float32, mybir.dt.float32r
F16, BF16 = mybir.dt.float16, mybir.dt.bfloat16
ALU = mybir.AluOpType
ACT = mybir.ActivationFunctionType
AX_X = mybir.AxisListType.X

P = 128
S, E, H = 2048, 512, 16
NOPE, ROPE, VD, LORA, RANK = 128, 64, 128, 128, 8
QH, HALF = NOPE + ROPE, ROPE // 2
CH = 512
NT, NC, KE, QT = S // P, S // CH, E // P, CH // P
SCALE = QH ** -0.5
FIRST = [sum(QT * (i + 1) for i in range(c)) for c in range(NC + 1)]
HT = FIRST[NC]
BT = 2 * HT
LAG, AHEAD = 3, 22
Q_AT = ((12, 10), (18, 16), (23, 22), (37, 34))
ROW_AT = {5: 2, 19: 3, 28: 4, 32: 5}
NB = H // 2
NEG = -1.0e30
HEADROOM = float(np.log(32.0)) / SCALE
PERIOD = {"tile": BT, "unit": 2 * NC, "head": 2}


def where(tile):
    h, s = divmod(tile, HT)
    c = max(c for c in range(NC) if FIRST[c] <= s)
    return h, c, s - FIRST[c], h * NC + c


class Silent:
    def then_inc(self, *a, **k):
        return self
    matmul = transpose = activation = tensor_copy = tensor_tensor = tensor_scalar = then_inc
    tensor_reduce = tensor_tensor_reduce = scalar_tensor_tensor = reciprocal = memset = then_inc
    bn_stats = bn_aggr = affine_select = dma_start = wait_ge = then_inc


class Counts:

    def __init__(self, sems):
        self.sems = sems
        self.at = {(part, s): {} for part in ("pre", "body", "last") for s in sems}
        self.total = {k: 0 for k in self.at}
        self.dry, self.part, self.it, self.seen, self.own = True, None, 0, {}, None

    def bias(self, s):
        return max(0, self.total["body", s] - self.total["pre", s])

    def begin(self, part, it):
        self.part, self.it, self.seen = part, it, {}

    def inc(self, ins, s, key, n=1):
        if self.dry:
            self.total[self.part, s] += n
            self.at[self.part, s][key] = self.total[self.part, s]
        ins.then_inc(self.sems[s], n)

    def wait(self, eng, s, key):
        if self.dry:
            return
        name, scope, index = key[:3]
        earlier = (name, scope, index + PERIOD[scope]) + tuple(key[3:])
        pre, body = self.total["pre", s], self.total["body", s]
        here = self.at[self.part, s]
        if self.part == "pre":
            if index < 0 and key not in here:
                return
            if key not in here:
                raise KeyError((s, key))
            offset, done = self.bias(s), here[key]
        else:
            offset = self.bias(s) + pre
            if key in here:
                done = here[key]
            elif earlier in self.at["body", s]:
                done = self.at["body", s][earlier] - body
            else:
                raise KeyError((self.part, s, key))
        if self.seen.get(s, -10 ** 9) >= done:
            return
        self.seen[s] = done
        if self.part == "body":
            eng.wait_ge(self.sems[s], self.it * body + (offset + done))
            if self.own:
                eng.sem_inc(self.own, 1)
        else:
            eng.wait_ge(self.sems[s], offset + done + (body * (NB - 1) if self.part == "last" else 0))

    def wait_all(self, eng, part):
        for s in self.sems:
            if part == "pre" and s in ("S", "G", "PV", "exp", "Ph", "Pl", "sum", "max"):
                continue
            n = self.bias(s) + self.total["pre", s]
            if part == "last":
                n += body_n(self, s)
            if n:
                eng.wait_ge(self.sems[s], n)


def body_n(counts, s):
    return counts.total["body", s] * (NB - 1) + counts.total["last", s]


def build(nc, x, wq, wkv_a, wkv_b, wo, kvs, factors, bias, rope_t, rope_n, out):
    ctx = ExitStack()
    with ctx:
        def sb(name, shape, dt):
            return ctx.enter_context(nc.sbuf_tensor(name, shape, dt))

        xTh = sb("xTh", [P, KE, S], F32R)
        xTl = sb("xTl", [P, KE, S], F32R)
        kTh = sb("kTh", [P, S], F32R)
        kTl = sb("kTl", [P, S], F32R)
        kR4 = sb("kR4", [P, S], F32R)
        kR5 = sb("kR5", [P, S], F32R)
        vH = sb("vH", [P, NT, LORA], F16)
        vL = sb("vL", [P, NT, LORA], F16)
        acc = sb("acc", [P, NT, E], F32)
        q = sb("q", [P, NC, 4, CH], F32R)
        wAbs = [sb(f"wAbs{i}", [P, KE, LORA], F32R) for i in range(2)]
        wPe = [sb(f"wPe{i}", [P, KE, P], F32R) for i in range(2)]
        wVo = [sb(f"wVo{i}", [P, E], F32R) for i in range(2)]
        wX = [sb(f"wX{i}", [P, KE, P], F32R) for i in range(2)]
        wKT = [sb(f"wKT{i}", [P, LORA], F32R) for i in range(2)]
        wVT = [sb(f"wVT{i}", [P, LORA], F32R) for i in range(2)]
        wst = sb("wst", [P, KE, P], F32)
        wkv = sb("wkv", [P, 2 * P], F32)
        tab = sb("tab", [P, 2, CH], F32)
        ex = sb("ex", [P, 2, CH], F32)
        pH = sb("pH", [P, 4, CH], F16)
        pL = sb("pL", [P, 4, CH], F16)
        esum = sb("esum", [P, 2, CH], F32)
        oH = sb("oH", [P, CH], F32R)
        oL = sb("oL", [P, CH], F32R)
        junk = sb("junk", [P, CH], BF16)
        gmax = sb("gmax", [P, NC, QT * NC], F32)
        rmax = sb("rmax", [P, 2, 2, QT], F32)
        rden = sb("rden", [P, QT], F32)
        ident = sb("ident", [P, P], F32)
        cmask = sb("cmask", [P, CH], BF16)
        ones = sb("ones", [P, 1], F16)
        eps = sb("eps", [P, 2], F32)
        scl = sb("scl", [P, 1], F32)
        ropen = sb("ropen", [P, NT, 2, HALF], F32)
        stats = sb("stats", [P, NT, 6], F32)
        mv = sb("mv", [P, NT, 2], F32)
        rstd = sb("rstd", [P, 3, NT], F32)
        ssq = sb("ssq", [P, 3, NT], F32)
        ps = ctx.enter_context(nc.psum_tensor("ps", [P, 8, CH], F32))
        SB, GB, OB, MB = 0, 2, 4, 6

        wa_f = vH[:, :, :].rearrange("p t n -> p (t n)").bitcast(F32)[:, 0:KE * QH].rearrange(
            "p (k n) -> p k n", k=KE)
        fsumA = pH[:, :, :].rearrange("p a n -> p (a n)").bitcast(F32).rearrange("p (k n) -> p k n", k=2)
        fsumB = pL[:, :, :].rearrange("p a n -> p (a n)").bitcast(F32).rearrange("p (k n) -> p k n", k=2)
        fsum = [fsumA[:, 0, :], fsumA[:, 1, :], fsumB[:, 0, :], fsumB[:, 1, :]]
        wa = [q[:, 1, :, :].rearrange("p a n -> p (a n)")[:, i * KE * QH:(i + 1) * KE * QH].rearrange(
            "p (k n) -> p k n", k=KE) for i in range(2)]
        facbuf = [ex[:, 0, :], ex[:, 1, :], wst[:, :, :].rearrange("p k n -> p (k n)")]
        ff = [q[:, 2 + i, :, :] for i in range(2)]
        kt = [tab[:, i, :].rearrange("p (t n) -> p t n", t=2) for i in range(2)]
        biasb = ex[:, 0, :]
        ktmp = junk[:, 2 * P:4 * P].bitcast(F32).rearrange("p (a t n) -> p a t n", a=2, t=2)
        sH, sL = [ropen[:, :, :, :].rearrange("p t a n -> p (t a n)").bitcast(F16)[:, i * CH:(i + 1) * CH]
                  for i in range(2)]
        stash = nc.dram_tensor("rope_stash", [NC, 2, P, CH], F32).ap()

        names = ["S", "G", "PV", "M",
                 "exp", "hi", "Ph",
                 "sum", "max", "free",
                 "Pl", "pool",
                 "d_wst", "d_wkv", "d_tab", "d_tab1", "d_x0", "d_x1", "d_w", "d_wa", "d_c", "d_stash", "d_out"]
        names += [f"d_f{i}" for i in range(3)] + [f"d_q{c}" for c in range(NC)]
        sems = {n: ctx.enter_context(nc.semaphore("s_" + n)) for n in names}
        cn = Counts(sems)
        idle = {w: ctx.enter_context(nc.semaphore("idle_" + w)) for w in ("dve", "pool", "sp")}
        wait, inc = cn.wait, cn.inc
        misc, bank_of = {"n": 0}, {}

        def f(ap):
            return ap.bitcast(F32)

        def three(e, o, a, b, first=True, last=True):
            e.matmul(o, a[0], b[0], start=first, stop=False)
            e.matmul(o, a[0], b[1], start=False, stop=False)
            return e.matmul(o, a[1], b[0], start=False, stop=last)

        def bank(e, who, key, previous):
            if who == "pe":
                n = misc["n"] % len(previous)
                misc["n"] += 1
                if previous[n] is not None:
                    wait(e, "free", previous[n])
                previous[n] = key
                bank_of[cn.part, key] = [MB, MB + 1, OB, OB + 1][n]
            return ps[:, bank_of[cn.part, key], :]

        prev = {"v": [None, None]}

        def split(e, who, key, src, hi, lo):
            if who == "act":
                wait(e, "M", key)
                inc(e.activation(hi, src, ACT.Copy), "hi", key)
            if who == "dve":
                wait(e, "hi", key)
                inc(e.tensor_tensor(lo, src, f(hi), ALU.subtract), "free", key)

        def constants(e, who):
            k = ("const", "unit", 0)
            if who == "pool":
                e.memset(ones[:, :], 1.0)
                e.memset(eps[:, 0:1], 1e-5)
                e.memset(eps[:, 1:2], 1e-6)
                e.memset(cmask[:, :], 0.0)
                inc(e.memset(ident[:, :], 0.0), "pool", ("zero", "unit", 0))
                wait(e, "pool", ("zero", "unit", 0))
                e.affine_select(out=ident[:, :], in_=ident[:, :], compare_op=ALU.not_equal, fill=1.0,
                                base=0, pattern=[[-1, P]], channel_multiplier=1)
                inc(e.affine_select(out=cmask[:, :], in_=cmask[:, :], compare_op=ALU.is_ge, fill=NEG,
                                    base=CH - P, pattern=[[-1, CH]], channel_multiplier=1), "pool", k)
            if who == "act":
                wait(e, "pool", ("zero", "unit", 0))
                e.activation(ssq[:, 0, 0:1], eps[:, 0:1], ACT.Sqrt, bias=eps[:, 0:1])
            if who == "dve":
                inc(e.memset(f(kR5[HALF * 2:HALF * 3, :]), 1.0), "free", k)

        def load_x(e, who, p2):
            if who == "sp":
                wait(e, f"d_x{p2 % 2}", ("x", "unit", p2 - 2))
                inc(e.dma_start(acc[:, 2 * p2:2 * p2 + 2, :],
                                x[2 * p2 * P:(2 * p2 + 2) * P, :].rearrange("(t p) n -> p t n", p=P)),
                    f"d_x{p2 % 2}", ("x", "unit", p2), 16)

        def load_wa(e, who):
            if who == "sp":
                inc(e.dma_start(wa_f, wkv_a.rearrange("(k p) n -> p k n", p=P)), "d_wa",
                    ("ld", "unit", 0), 16)

        def load_tables(e, who):
            k = ("ld", "unit", 0)
            if who == "sp":
                inc(e.dma_start(ropen[:, :, :, :], rope_n), "d_c", k, 16)

        def load_bias(e, who):
            k = ("bias", "unit", 0)
            if who == "sp":
                wait(e, "pool", ("fac", "unit", RANK * KE - 1))
                inc(e.dma_start(biasb, bias.rearrange("(a n) -> a n", a=1).broadcast_to([P, E])), "d_c", k, 16)

        def cn_add(s, key, n):
            if cn.dry:
                cn.total[cn.part, s] += n
                cn.at[cn.part, s][key] = cn.total[cn.part, s]

        def split_wa(e, who):
            k = ("wa", "unit", 0)
            if who == "act":
                wait(e, "d_wa", ("ld", "unit", 0))
                inc(e.activation(wa[0], wa_f, ACT.Copy), "hi", k)
            if who == "dve":
                wait(e, "hi", k)
                inc(e.tensor_tensor(wa[1], wa_f, f(wa[0]), ALU.subtract), "free", k)

        def norm_stats(e, who, p2):
            ts = slice(2 * p2, 2 * p2 + 2)
            if who == "dve":
                wait(e, f"d_x{p2 % 2}", ("x", "unit", p2))
                for t in range(2 * p2, 2 * p2 + 2):
                    ins = e.bn_stats(stats[:, t, :], acc[:, t, :])
                inc(ins, "free", ("bn", "unit", p2))
                wait(e, "free", ("bn", "unit", p2))
                for t in range(2 * p2, 2 * p2 + 2):
                    ins = e.bn_aggr(mv[:, t, :], stats[:, t, :])
                inc(ins, "free", ("var", "unit", p2))

        def norm_scale(e, who, p2):
            ts = slice(2 * p2, 2 * p2 + 2)
            if who == "act":
                wait(e, "pool", ("const", "unit", 0))
                wait(e, "free", ("var", "unit", p2))
                inc(e.activation(rstd[:, 0, ts], mv[:, ts, 1], ACT.Sqrt, bias=eps[:, 0:1]), "hi",
                    ("sd", "unit", p2))
            if who == "dve":
                wait(e, "hi", ("sd", "unit", p2))
                inc(e.reciprocal(rstd[:, 1, ts], rstd[:, 0, ts]), "free", ("rstd", "unit", p2))
                wait(e, "free", ("rstd", "unit", p2))
                inc(e.scalar_tensor_tensor(out=rstd[:, 2, ts], in0=mv[:, ts, 0], scalar=-1.0,
                                           in1=rstd[:, 1, ts], op0=ALU.mult, op1=ALU.mult), "free",
                    ("nmr", "unit", p2))

        def normalize(e, who, t):
            if who == "act":
                wait(e, "free", ("nmr", "unit", t // 2))
                wait(e, "M", ("xt", "unit", t - 2))
                inc(e.activation(esum[:, t % 2, :], acc[:, t, :], ACT.Identity,
                                 bias=rstd[:, 2, t:t + 1], scale=rstd[:, 1, t:t + 1]), "hi",
                    ("xn", "unit", t))

        def transpose_x(e, who, t):
            k = ("xt", "unit", t)
            b = bank(e, who, k, prev["v"])
            xn = esum[:, t % 2, :]
            if who == "pe":
                wait(e, "pool", ("const", "unit", 0))
                wait(e, "hi", ("xn", "unit", t))
                for k4 in range(KE):
                    ins = e.transpose(b[:, k4 * P:(k4 + 1) * P], xn[:, k4 * P:(k4 + 1) * P], ident[:, :])
                inc(ins, "M", k)
            cols = slice(t * P, t * P + P)
            split(e, who, k, b.rearrange("p (k n) -> p k n", k=KE), xTh[:, :, cols], xTl[:, :, cols])

        def add_bias(e, who, t):
            if who == "pool":
                wait(e, "d_c", ("bias", "unit", 0))
                wait(e, "hi", ("xn", "unit", t))
                inc(e.tensor_tensor(acc[:, t, :], acc[:, t, :], biasb, ALU.add), "pool",
                    ("bias", "unit", t))

        def latent_bank(p2):
            return ps[:, SB + p2 % 2, 0:2 * QH].rearrange("p (t n) -> p t n", t=2)

        def latent_product(e, who, t):
            if who == "pe":
                wait(e, "free", ("wa", "unit", 0))
                wait(e, "free", ("kva", "unit", t // 2 - 2))
                wait(e, "free", ("xt", "unit", t))
                cols = slice(t * P, (t + 1) * P)
                for k4 in range(KE):
                    ins = three(e, latent_bank(t // 2)[:, t % 2, :], [xTh[:, k4, cols], xTl[:, k4, cols]],
                                [wa[0][:, k4, :], wa[1][:, k4, :]], k4 == 0, k4 == KE - 1)
                inc(ins, "M", ("kva", "unit", t // 2) if t % 2 else ("kva1", "unit", t // 2))

        def latent(e, who, p2):
            k = ("kva", "unit", p2)
            b = latent_bank(p2)
            ts = slice(2 * p2, 2 * p2 + 2)
            cos, sin = ropen[:, ts, 0, :], ropen[:, ts, 1, :]
            lo, hi = b[:, :, LORA:LORA + HALF], b[:, :, LORA + HALF:QH]
            kk = kt[p2 % 2]
            r1, r2 = kk[:, :, LORA:LORA + HALF], kk[:, :, LORA + HALF:LORA + ROPE]
            if who == "act":
                wait(e, "M", k)
                for i in range(2):
                    if 2 * p2 + i:
                        wait(e, "hi", ("sq", "unit", 2 * p2 + i - 1))
                    inc(e.activation(junk[:, 0:LORA], b[:, i, 0:LORA], ACT.Square,
                                     accum_out=ssq[:, 0, 2 * p2 + i:2 * p2 + i + 1]), "hi",
                        ("sq", "unit", 2 * p2 + i))
                wait(e, "hi", ("sq", "unit", 2 * p2 + 1))
                inc(e.activation(ssq[:, 1, ts], ssq[:, 0, ts], ACT.Sqrt, bias=eps[:, 1:2],
                                 scale=1.0 / LORA), "hi", ("rms", "unit", p2))
            if who == "dve":
                wait(e, "d_c", ("ld", "unit", 0))
                wait(e, "hi", ("rms", "unit", p2))
                inc(e.reciprocal(ssq[:, 2, ts], ssq[:, 1, ts]), "free", ("rr", "unit", p2))
                if p2 >= 2:
                    wait(e, "M", ("kT", "unit", p2 - 2))
                    wait(e, "free", ("vL", "unit", p2 - 2))
                wait(e, "free", ("rr", "unit", p2))
                for i in range(2):
                    e.tensor_scalar(kk[:, i, 0:LORA], b[:, i, 0:LORA], ssq[:, 2, 2 * p2 + i:2 * p2 + i + 1],
                                    None, ALU.mult)
                e.tensor_tensor(r1, lo, cos, ALU.mult)
                e.tensor_tensor(ktmp[:, 0, :, :], hi, sin, ALU.mult)
                e.tensor_tensor(r2, hi, cos, ALU.mult)
                inc(e.tensor_tensor(ktmp[:, 1, :, :], lo, sin, ALU.mult), "free", k)
                wait(e, "free", k)
                e.tensor_tensor(r1, r1, ktmp[:, 0, :, :], ALU.subtract)
                inc(e.tensor_tensor(r2, r2, ktmp[:, 1, :, :], ALU.add), "free", ("rope", "unit", p2))
                wait(e, "free", ("rope", "unit", p2))
                inc(e.tensor_copy(kk[:, :, LORA + ROPE:2 * P], kk[:, :, LORA:LORA + ROPE]), "free",
                    ("kk", "unit", p2))

        def value_parts(e, who, p2):
            kk, ts = kt[p2 % 2], slice(2 * p2, 2 * p2 + 2)
            if who == "act":
                wait(e, "free", ("kk", "unit", p2))
                inc(e.activation(vH[:, ts, :], kk[:, :, 0:LORA], ACT.Copy), "hi", ("vH", "unit", p2))
            if who == "dve":
                wait(e, "hi", ("vH", "unit", p2))
                inc(e.tensor_tensor(vL[:, ts, :], kk[:, :, 0:LORA], vH[:, ts, :], ALU.subtract), "free",
                    ("vL", "unit", p2))

        def keys(e, who, p2):
            k = ("kT", "unit", p2)
            b = bank(e, who, k, prev["v"])
            kk = kt[p2 % 2]
            cols = slice(2 * p2 * P, (2 * p2 + 2) * P)
            if who == "pe":
                wait(e, "free", ("kk", "unit", p2))
                for i in range(2):
                    e.transpose(b[:, i * P:(i + 1) * P], kk[:, i, 0:P], ident[:, :])
                    ins = e.transpose(b[:, (2 + i) * P:(3 + i) * P], kk[:, i, P:2 * P], ident[:, :])
                inc(ins, "M", k)
            if who == "act":
                wait(e, "M", k)
                e.activation(kTh[:, cols], b[:, 0:2 * P], ACT.Copy)
                inc(e.activation(kR4[:, cols], b[:, 2 * P:4 * P], ACT.Copy), "hi", k)
            if who == "dve":
                wait(e, "hi", k)
                e.tensor_tensor(kTl[:, cols], b[:, 0:2 * P], f(kTh[:, cols]), ALU.subtract)
                inc(e.tensor_tensor(kR5[0:ROPE, cols], b[0:ROPE, 2 * P:4 * P], f(kR4[0:ROPE, cols]),
                                    ALU.subtract), "free", k)

        def factor(e, who, i):
            r, k4 = divmod(i, KE)
            k = ("fac", "unit", i)
            n = (i - KE) % 3
            src = factors[r, k4 * P:(k4 + 1) * P, :]
            if r == 0:
                if who == "sp":
                    ins = e.dma_start(fsum[k4], src)
                    ins.then_inc(sems["d_w"], 16)
                    cn_add("d_w", k, 16)
                return
            if who == "sp":
                if i == KE + 2:
                    wait(e, "M", ("tq", "head", 0))
                if i >= KE + 3:
                    wait(e, "pool", ("fac", "unit", i - 3))
                inc(e.dma_start(facbuf[n], src), f"d_f{n}", k, 16)
            if who == "pool":
                wait(e, "d_w", ("fac", "unit", KE - 1))
                wait(e, f"d_f{n}", k)
                if r > 1:
                    wait(e, "pool", ("fac", "unit", i - KE))
                inc(e.tensor_tensor(fsum[k4], fsum[k4], facbuf[n], ALU.add), "pool", k)

        def split_ff(e, who):
            for k4 in range(KE):
                k = ("ff", "unit", k4)
                if who == "act":
                    wait(e, "pool", ("fac", "unit", RANK * KE - KE + k4))
                    inc(e.activation(ff[0][:, k4, :], fsum[k4], ACT.Copy), "hi", k)
                if who == "dve":
                    wait(e, "hi", k)
                    inc(e.tensor_tensor(ff[1][:, k4, :], fsum[k4], f(ff[0][:, k4, :]), ALU.subtract),
                        "free", k)

        def ffn(e, who, t):
            k = ("ffn", "unit", t)
            b = bank(e, who, k, prev["v"])
            cols = slice(t * P, t * P + P)
            if who == "pe":
                wait(e, "free", ("xt", "unit", t))
                wait(e, "free", ("ff", "unit", KE - 1))
                for k4 in range(KE):
                    ins = three(e, b, [xTh[:, k4, cols], xTl[:, k4, cols]],
                                [ff[0][:, k4, :], ff[1][:, k4, :]], k4 == 0, k4 == KE - 1)
                inc(ins, "M", k)
            if who == "dve":
                wait(e, "M", k)
                wait(e, "pool", ("bias", "unit", t))
                inc(e.scalar_tensor_tensor(out=acc[:, t, :], in0=b, scalar=float(RANK) ** -0.5,
                                           in1=acc[:, t, :], op0=ALU.mult, op1=ALU.add), "free", k)

        def head0():
            return cn.it * 2

        def load(e, who, kind, h, after):
            if who != "sp":
                return
            if after:
                wait(e, after[0], after[1])
            k = ("w" + kind, "head", h)
            wqv = wq.rearrange("(k p) n -> p k n", p=P)
            hh = head0() + h
            if kind == "q":
                inc(e.dma_start(wst[:, :, :], wqv[:, :, bass.ds(hh * QH, NOPE)]), "d_wst", k, 16)
            if kind == "o":
                inc(e.dma_start(wst[:, :, :], wo[bass.ds(hh * VD, VD), :].rearrange(
                    "p (k n) -> p k n", k=KE)), "d_wst", k, 16)
            if kind == "pe":
                for half in range(2):
                    for b in range(2):
                        at = (2 * half + b) * HALF
                        ins = e.dma_start(wst[:, :, at:at + HALF],
                                          wqv[:, :, bass.ds(hh * QH + b * QH + NOPE + half * HALF, HALF)])
                        inc(ins, "d_wst", k, 16)

        def load_kv(e, who, h, first=False):
            if who == "sp":
                if first:
                    e.dma_start(scl[:, :], kvs.rearrange("(p a) -> p a", a=1)).then_inc(sems["d_wkv"], 16)
                    cn_add("d_wkv", ("wkv", "head", h), 16)
                else:
                    wait(e, "M", ("wvt", "head", h - 1))
                inc(e.dma_start(wkv[:, :], wkv_b[:, bass.ds((head0() + h) * 2 * P, 2 * P)]), "d_wkv",
                    ("wkv", "head", h), 16)

        def scale_kv(e, who, h):
            if who == "dve":
                wait(e, "d_wkv", ("wkv", "head", h))
                inc(e.tensor_scalar(wkv[:, :], wkv[:, :], scl[:, 0:1], None, ALU.mult), "free",
                    ("kvs", "head", h))

        def wq_transpose(e, who, h):
            k = ("tq", "head", h)
            b = bank(e, who, k, prev["v"])
            if who == "pe":
                if cn.part == "pre":
                    wait(e, "pool", ("const", "unit", 0))
                wait(e, "d_wst", ("wq", "head", h))
                for k4 in range(KE):
                    ins = e.transpose(b[:, k4 * P:(k4 + 1) * P], wst[:, k4, :], ident[:, :])
                inc(ins, "M", k)
            if who == "act":
                wait(e, "M", ("wvo", "head", h - 1))
            split(e, who, k, b.rearrange("p (k n) -> p k n", k=KE), wX[0][:, :, :], wX[1][:, :, :])

        def wk_transpose(e, who, h):
            k = ("tk", "head", h)
            b = bank(e, who, k, prev["v"])[:, 0:P]
            if who == "pe":
                wait(e, "free", ("kvs", "head", h))
                inc(e.transpose(b, wkv[:, 0:P], ident[:, :]), "M", k)
            split(e, who, k, b, wKT[0][:, :], wKT[1][:, :])

        def w_abs(e, who, h):
            k = ("wabs", "head", h)
            b = bank(e, who, k, prev["v"])
            if who == "pe":
                wait(e, "free", ("tq", "head", h))
                wait(e, "free", ("tk", "head", h))
                for k4 in range(KE):
                    ins = three(e, b[:, k4 * P:(k4 + 1) * P], [w[:, k4, :] for w in wX],
                                [w[:, :] for w in wKT])
                inc(ins, "M", k)
            split(e, who, k, b.rearrange("p (k n) -> p k n", k=KE), wAbs[0][:, :, :], wAbs[1][:, :, :])

        def w_pe(e, who, h):
            k = ("pew", "head", h)
            if who == "act":
                wait(e, "d_wst", ("wpe", "head", h))
                if cn.part != "pre":
                    wait(e, "M", ("pe", "unit", (h - 2) * NC + NC - 1))
                inc(e.activation(wPe[0][:, :, :], wst[:, :, :], ACT.Copy), "hi", k)
            if who == "dve":
                wait(e, "hi", k)
                inc(e.tensor_tensor(wPe[1][:, :, :], wst[:, :, :], f(wPe[0][:, :, :]), ALU.subtract),
                    "free", k)

        def wv_transpose(e, who, h):
            k = ("wvt", "head", h)
            b = bank(e, who, k, prev["v"])[:, 0:P]
            if who == "pe":
                wait(e, "free", ("kvs", "head", h))
                inc(e.transpose(b, wkv[:, P:2 * P], ident[:, :]), "M", k)
            split(e, who, k, b, wVT[0][:, :], wVT[1][:, :])

        def w_o(e, who, h):
            k = ("wos", "head", h)
            if who == "act":
                wait(e, "d_wst", ("wo", "head", h))
                wait(e, "M", ("wabs", "head", h))
                inc(e.activation(wX[0][:, :, :], wst[:, :, :], ACT.Copy), "hi", k)
            if who == "dve":
                wait(e, "hi", k)
                inc(e.tensor_tensor(wX[1][:, :, :], wst[:, :, :], f(wX[0][:, :, :]), ALU.subtract),
                    "free", k)

        def w_vo(e, who, h):
            k = ("wvo", "head", h)
            b = bank(e, who, k, prev["v"])
            if who == "pe":
                wait(e, "free", ("wos", "head", h))
                wait(e, "free", ("wvt", "head", h))
                ins = three(e, b, [w[:, :] for w in wVT], [w[:, :, :].rearrange("p k n -> p (k n)") for w in wX])
                inc(ins, "M", k)
            split(e, who, k, b, wVo[0][:, :], wVo[1][:, :])

        def q_latent(e, who, u):
            h, c = divmod(u, NC)
            k = ("q", "unit", u)
            b = bank(e, who, k, prev["v"])
            cols = slice(c * CH, c * CH + CH)
            if who == "pe":
                wait(e, "free", ("wabs", "head", h))
                for k4 in range(KE):
                    ins = three(e, b, [w[:, k4, :] for w in wAbs], [xTh[:, k4, cols], xTl[:, k4, cols]],
                                k4 == 0, k4 == KE - 1)
                inc(ins, "M", k)
            if who == "act":
                wait(e, "S", last_tile(u - NC))
            split(e, who, k, b, q[:, c, 0, :], q[:, c, 1, :])

        def last_tile(u):
            h, c = divmod(u, NC)
            return ("s", "tile", h * HT + FIRST[c + 1] - 1)

        def table(u):
            return esum[:, :, :] if cn.part == "pre" and u % 2 else tab[:, :, :]

        def d_table(u):
            return "d_tab1" if cn.part == "pre" and u % 2 else "d_tab"

        def load_table(e, who, u, *after):
            if who == "sp":
                for a in after:
                    wait(e, *a)
                c = u % NC
                inc(e.dma_start(table(u), rope_t[:, :, c * CH:(c + 1) * CH]), d_table(u),
                    ("tab", "unit", u), 16)

        def q_rope(e, who, u):
            h, c = divmod(u, NC)
            k = ("pe", "unit", u)
            b = bank(e, who, k, prev["v"])
            cols = slice(c * CH, c * CH + CH)
            cos, sin = table(u)[:, 0, :], table(u)[:, 1, :]
            if who == "pe":
                wait(e, "free", ("pew", "head", h))
                for k4 in range(KE):
                    ins = three(e, b, [w[:, k4, :] for w in wPe], [xTh[:, k4, cols], xTl[:, k4, cols]],
                                k4 == 0, k4 == KE - 1)
                inc(ins, "M", k)
            if who == "dve":
                wait(e, d_table(u), ("tab", "unit", u))
                wait(e, "M", k)
                e.tensor_tensor(cos, b, cos, ALU.mult)
                e.tensor_tensor(sin[0:ROPE, :], b[ROPE:P, :], sin[0:ROPE, :], ALU.mult)
                inc(e.tensor_tensor(sin[ROPE:P, :], b[0:ROPE, :], sin[ROPE:P, :], ALU.mult), "free", k)
            if who == "pool":
                wait(e, "free", k)
                inc(e.tensor_tensor(cos, cos, sin, ALU.add), "pool", ("ro", "unit", u))

        def rope_parts(e, who, u):
            h, c = divmod(u, NC)
            k = ("pe", "unit", u)
            cos, sin = table(u)[:, 0, :], table(u)[:, 1, :]
            if who == "pool":
                wait(e, "hi", k)
                inc(e.tensor_tensor(cos, cos, sin, ALU.subtract), "pool", k)
            if who == "act":
                wait(e, "pool", ("ro", "unit", u))
                inc(e.activation(sin.bitcast(F32R), cos, ACT.Copy), "hi", k)
            if who == "sp":
                wait(e, "pool", k)
                if cn.part != "pre":
                    wait(e, f"d_q{c}", ("qr", "unit", u - NC))
                inc(e.dma_start(stash[c].rearrange("a p n -> p a n"), table(u)), "d_stash", k, 16)
                if cn.part == "pre" and c > 1:
                    return
                wait(e, "S", last_tile(u - NC))
                fill(e, u, [table(u)[:, i, :] for i in range(2)], 0)

        def fill_late(e, who, c):
            if who == "sp":
                wait(e, "d_stash", ("pe", "unit", c))
                wait(e, "M", ("ffn", "unit", NT - 1))
                fill(e, c, [stash[c, i] for i in range(2)], 0)

        def fill(e, u, lohi, b):
            c = u % NC
            lo, hi = lohi
            for half in range(2):
                src = slice((2 * half + b) * HALF, (2 * half + b + 1) * HALF)
                dst = half * HALF
                e.dma_start(f(q[dst:dst + HALF, c, 2, :]), hi[src, :]).then_inc(sems[f"d_q{c}"], 16)
                e.dma_start(f(q[dst:dst + HALF, c, 3, :]), hi[src, :]).then_inc(sems[f"d_q{c}"], 16)
                cn_add(f"d_q{c}", None, 32)
                inc(e.dma_start(f(q[ROPE + dst:ROPE + dst + HALF, c, 2, :]), lo[src, :]), f"d_q{c}",
                    ("qr", "unit", u), 16)

        def q_rope_second(e, who, u):
            if who == "sp":
                wait(e, "d_stash", ("pe", "unit", u - NC))
                wait(e, "S", last_tile(u - NC))
                fill(e, u, [stash[u % NC, i] for i in range(2)], 1)

        def group(e, who, g):
            h, c, j, u = where(g)
            t, kg = divmod(j, c + 1)
            k = ("g", "tile", g)
            n = CH if kg < c else (t + 1) * P
            b = ps[:, GB + g % 2, 0:n]
            qs, ks = slice(t * P, t * P + P), slice(kg * CH, kg * CH + n)
            m = gmax[:, u % NC, t * NC + kg:t * NC + kg + 1]
            if who == "pe":
                wait(e, "max", ("g", "tile", g - 2))
                if j == 0:
                    wait(e, "free", ("q", "unit", u))
                e.matmul(b, q[:, c, 0, qs], kTh[:, ks], start=True, stop=False)
                if j == 0:
                    wait(e, f"d_q{c}", ("qr", "unit", u))
                inc(e.matmul(b, q[0:ROPE, c, 2, qs], kR4[0:ROPE, ks], start=False, stop=True), "G", k)
            if who == "dve":
                wait(e, "max", ("g", "tile", g - 1))
                wait(e, "G", k)
                if kg < c:
                    inc(e.tensor_reduce(m, b, AX_X, ALU.max), "max", k)
                else:
                    if cn.part == "body" and not cn.dry:
                        e.sem_inc(idle["dve"], 1)
                    inc(e.tensor_tensor_reduce(out=junk[:, 0:n], in0=b, in1=cmask[:, CH - n:CH], scale=1.0,
                                               scalar=NEG, op0=ALU.add, op1=ALU.max, accum_out=m), "max", k)

        def max_column(e, who, u):
            h, c = divmod(u, NC)
            gm = gmax[:, u % NC, :].rearrange("p (t g) -> p t g", t=QT)[:, :, 0:c + 1]
            if who == "dve":
                wait(e, "max", ("g", "tile", h * HT + FIRST[c + 1] - 1))
                inc(e.tensor_reduce(rmax[:, u % 2, 0, :], gm, AX_X, ALU.max), "free", ("rm", "unit", u))
                wait(e, "free", ("rm", "unit", u))
                inc(e.tensor_scalar(rmax[:, u % 2, 1, :], rmax[:, u % 2, 0, :], -1.0, HEADROOM, ALU.mult, ALU.add),
                    "free", ("nm", "unit", u))

        def max_row(e, who, u):
            h, c = divmod(u, NC)
            k = ("mT", "unit", u)
            b = bank(e, who, k, prev["v"])[0:QT, 0:P]
            if who == "dve":
                wait(e, "M", k)
                qq = q[ROPE:ROPE + QT, c, 3, :].rearrange("p (t n) -> p t n", t=QT)
                inc(e.tensor_tensor(qq, b.unsqueeze(1).broadcast_to([QT, QT, P]),
                                    ident[0:QT, 0:QT].unsqueeze(2).broadcast_to([QT, QT, P]), ALU.mult),
                    "free", k)
            if who == "pe":
                wait(e, "free", ("nm", "unit", u))
                inc(e.transpose(b, rmax[:, u % 2, 1, :], ident[:, :]), "M", k)

        def scores(e, who, T):
            h, c, j, u = where(T)
            k = ("s", "tile", T)
            n0 = max(0, j - QT * c) * P
            b = ps[:, SB + T % 2, n0:CH]
            ks = slice(j * P, j * P + P)
            x2, x4 = T % 2, T % 4
            diagonal = j >= QT * c
            if who == "pe":
                wait(e, "exp", ("s", "tile", T - 2))
                if j == 0:
                    wait(e, "free", ("mT", "unit", u))
                three(e, b, [kTh[:, ks], kTl[:, ks]], [q[:, c, 0, n0:], q[:, c, 1, n0:]], True, False)
                e.matmul(b, kR4[:, ks], q[:, c, 2, n0:], start=False, stop=False)
                inc(e.matmul(b, kR5[0:ROPE + QT, ks], q[0:ROPE + QT, c, 3, n0:], start=False, stop=True),
                    "S", k)
            if who == "act":
                wait(e, "sum", ("s", "tile", T - 2))
                wait(e, "Pl", ("s", "tile", T - 2))
                wait(e, "S", k)
                inc(e.activation(ex[:, x2, n0:], b, ACT.Exp, scale=SCALE), "exp", k)
                wait(e, "PV", ("s", "tile", T - 4))
                if diagonal:
                    wait(e, "pool", ("mask", "tile", T))
                else:
                    wait(e, "exp", k)
                inc(e.activation(pH[:, x4, n0:], ex[:, x2, n0:], ACT.Copy), "Ph", k)
            if who == "pool":
                if diagonal:
                    wait(e, "exp", k)
                    if cn.part == "body" and not cn.dry:
                        e.sem_inc(idle["pool"], 1)
                    blk = ex[:, x2, n0:n0 + P]
                    inc(e.affine_select(out=blk, in_=blk, compare_op=ALU.is_ge, fill=0.0, base=0,
                                        pattern=[[1, P]], channel_multiplier=-1), "pool", ("mask", "tile", T))
                wait(e, "Ph", k)
                inc(e.tensor_tensor(pL[:, x4, n0:], ex[:, x2, n0:], pH[:, x4, n0:], ALU.subtract), "Pl", k)

        def row_sum(e, who, T):
            h, c, j, u = where(T)
            n0 = max(0, j - QT * c) * P
            if who == "dve":
                k = ("s", "tile", T)
                if j >= QT * c:
                    wait(e, "pool", ("mask", "tile", T))
                else:
                    wait(e, "exp", k)
                es = esum[:, u % 2, n0:]
                if j == 0:
                    wait(e, "pool", ("es", "unit", u - 2))
                    if cn.part == "pre":
                        wait(e, "d_stash", ("pe", "unit", NC - 1))
                    inc(e.tensor_copy(es, ex[:, T % 2, n0:]), "sum", k)
                else:
                    wait(e, "sum", ("s", "tile", T - 1))
                    inc(e.tensor_tensor(es, es, ex[:, T % 2, n0:], ALU.add), "sum", k)

        def values(e, who, T):
            h, c, j, u = where(T)
            n0 = max(0, j - QT * c) * P
            if who == "pe":
                k = ("s", "tile", T)
                if j == 0:
                    wait(e, "free", ("o", "unit", u - 2))
                if T == 0 and cn.part == "pre":
                    for k0 in prev["v"][2:]:
                        wait(e, "free", k0)
                wait(e, "Pl", k)
                inc(three(e, ps[:, OB + u % 2, n0:], [vH[:, j, :], vL[:, j, :]],
                          [pH[:, T % 4, n0:], pL[:, T % 4, n0:]], j == 0, j == QT * (c + 1) - 1), "PV", k)

        def split_sums(e, who, u):
            h, c = divmod(u, NC)
            k = ("es", "unit", u)
            if who == "act":
                wait(e, "sum", ("s", "tile", h * HT + FIRST[c + 1] - 1))
                wait(e, "M", ("den", "unit", u - 1))
                inc(e.activation(sH, esum[:, u % 2, :], ACT.Copy), "hi", k)
            if who == "pool":
                wait(e, "hi", k)
                inc(e.tensor_tensor(sL, esum[:, u % 2, :], sH, ALU.subtract), "pool", k)

        def denominators(e, who, u):
            k = ("den", "unit", u)
            b = bank(e, who, k, prev["v"])[:, 0:QT]
            if who == "pe":
                wait(e, "pool", ("es", "unit", u))
                for t in range(QT):
                    qs = slice(t * P, (t + 1) * P)
                    e.matmul(b[:, t:t + 1], sH[:, qs], ones[:, :], start=True, stop=False)
                    ins = e.matmul(b[:, t:t + 1], sL[:, qs], ones[:, :], start=False, stop=True)
                inc(ins, "M", k)
            if who == "dve":
                wait(e, "M", k)
                inc(e.reciprocal(rden[:, :], b), "free", k)

        def read_output(e, who, u):
            h, c = divmod(u, NC)
            k = ("o", "unit", u)
            b = ps[:, OB + u % 2, :]
            if who == "act":
                wait(e, "PV", ("s", "tile", h * HT + FIRST[c + 1] - 1))
                wait(e, "M", ("out", "unit", u - 1, QT - 1))
                inc(e.activation(oH[:, :], b, ACT.Copy), "hi", k)
            if who == "dve":
                wait(e, "hi", k)
                inc(e.tensor_tensor(oL[:, :], b, f(oH[:, :]), ALU.subtract), "free", k)

        def head_output(e, who, u, t):
            h, c = divmod(u, NC)
            k = ("out", "unit", u, t)
            b = bank(e, who, k, prev["v"])
            if who == "pe":
                wait(e, "free", ("o", "unit", u))
                wait(e, "free", ("wvo", "head", h))
                inc(three(e, b, [oH[:, t * P:(t + 1) * P], oL[:, t * P:(t + 1) * P]], [w[:, :] for w in wVo]),
                    "M", k)
            a = acc[:, QT * c + t, :]
            if who == "dve":
                wait(e, "M", k)
                wait(e, "free", ("den", "unit", u))
                inc(e.scalar_tensor_tensor(out=a, in0=b, scalar=rden[:, t:t + 1], in1=a, op0=ALU.mult,
                                           op1=ALU.add), "free", k)
            if who == "sp" and cn.part == "last" and h == 1:
                wait(e, "free", k)
                inc(e.dma_start(out[(QT * c + t) * P:(QT * c + t + 1) * P, :], a), "d_out", k, 16)

        def prologue():
            NP = NT // 2
            yield constants,
            yield load_x, 0
            yield load, "q", 0, None
            yield load_kv, 0, True
            yield load_wa,
            yield load_x, 1
            yield load_x, 2
            facs = iter(range(RANK * KE))
            for _, i in zip(range(KE + 3), facs):
                yield factor, i
            yield load_tables,
            for p in range(3, NP):
                yield load_x, p
            yield norm_stats, 0
            yield scale_kv, 0
            yield wq_transpose, 0
            yield wk_transpose, 0
            yield norm_scale, 0
            yield normalize, 0
            yield norm_stats, 1
            yield norm_scale, 1
            for t in range(NT + 4):
                p = t // 2
                if t + 1 < NT:
                    yield normalize, t + 1
                if t % 2 == 0 and 0 <= p - 2 < NP:
                    yield "dve", latent, p - 2
                if t < NT:
                    yield transpose_x, t
                if t == 0:
                    yield split_wa,
                    yield w_abs, 0
                if t % 2 == 0 and 0 <= p - 2 < NP:
                    yield value_parts, p - 2
                if t < NT:
                    for _, i in zip(range(3), facs):
                        yield factor, i
                if t == NT - 4:
                    yield load, "pe", 0, ("pool", ("fac", "unit", RANK * KE - 2))
                if t == NT:
                    yield w_pe, 0
                    yield load, "o", 0, ("free", ("pew", "head", 0))
                if t % 2 == 1 and 0 <= p - 2 < NP:
                    yield keys, p - 2
                if 0 <= t - 2 < NT:
                    yield latent_product, t - 2
                if t % 2 == 1 and 0 <= p - 1 < NP:
                    yield "act", latent, p - 1
                if p + 2 < NP:
                    yield norm_stats if t % 2 == 0 else norm_scale, p + 2
            yield load_bias,
            yield load_table, 0, ("M", ("kT", "unit", NP - 1)), ("free", ("vL", "unit", NP - 1))
            yield load_table, 1, ("M", ("xt", "unit", NT - 1))
            ffs = iter(range(NT))

            def ffns(n):
                for _, t in zip(range(n), ffs):
                    yield add_bias, t
                    yield ffn, t

            yield wv_transpose, 0
            yield w_o, 0
            yield split_ff,
            for c in range(NC):
                yield q_rope, c
                if c < 2:
                    yield q_latent, c
                else:
                    yield max_row, c - 2
                yield rope_parts, c
                if c < NC - 1:
                    yield load_table, c + 2 if c < 2 else 2 * NC, \
                        (f"d_q{c}", ("qr", "unit", c)) if c < 2 else ("d_stash", ("pe", "unit", c))
                yield from ffns(2)
                if 0 < c < 3:
                    for g in range(FIRST[c - 1], FIRST[c]):
                        yield group, g
                        if g % 2:
                            yield from ffns(1)
                    yield max_column, c - 1
            yield from ffns(NT)
            yield load, "q", 1, ("free", ("wos", "head", 0))
            yield load_kv, 1
            for c in range(2, NC):
                yield q_latent, c
                yield fill_late, c
            for g in range(FIRST[2], AHEAD):
                yield group, g
            for T in range(LAG):
                yield scores, T
                if T:
                    yield row_sum, T - 1
            yield from slots(0, FIRST[1])

        def slots(first, end, last=False):
            late = []

            def task(step, *args):
                if sum(isinstance(x[0], str) for x in late) >= 2:
                    yield from late
                    late.clear()
                late.append(("act dve pool sp", step, *args))
                yield ("pe", step, *args)

            for T in range(first, end):
                h, c, j, u = where(T)
                s = T % HT
                more = not last or h == 0
                yield from late
                late.clear()
                for cc in range(NC):
                    if s == Q_AT[cc][1] + 2 and h == 1 and more:
                        yield rope_parts, 2 * NC + cc
                        yield load_table, 2 * NC + cc + 1 if cc < NC - 1 else 4 * NC, \
                            (f"d_q{cc}", ("qr", "unit", 2 * NC + cc))
                yield values, T
                if not last or T + LAG < BT:
                    yield scores, T + LAG
                if not last or T + AHEAD < BT:
                    yield group, T + AHEAD
                if not last or T + LAG - 1 < BT:
                    yield row_sum, T + LAG - 1
                for uu in range(2, 3 * NC):
                    hh, cc = divmod(uu, NC)
                    if not (last and uu >= 2 * NC):
                        if hh * HT + FIRST[cc + 1] == T + AHEAD:
                            yield max_column, uu
                if s in ROW_AT and not (last and h * NC + ROW_AT[s] >= 2 * NC):
                    yield from task(max_row, h * NC + ROW_AT[s])
                if u and j == 1:
                    yield from task(denominators, u - 1)
                if u and j in (2, 3):
                    for t in range(2 * j - 4, 2 * j - 2):
                        yield from task(head_output, u - 1, t)
                if j == QT * (c + 1) - 2:
                    yield split_sums, u
                if j == QT * (c + 1) - 1:
                    yield read_output, u
                if s == 4:
                    yield from task(w_vo, h)
                if more:
                    if s == 4:
                        yield scale_kv, h + 1
                        yield from task(wq_transpose, h + 1)
                        if h == 1:
                            yield load, "pe", 2, ("M", ("tq", "head", 2))
                        else:
                            yield load, "o", 1, ("M", ("tq", "head", 1))
                    if s == 8:
                        yield from task(wk_transpose, h + 1)
                    if s == 10:
                        yield from task(w_abs, h + 1)
                    if s == 8 and h == 1:
                        yield w_pe, 2
                        yield load, "o", 2, ("free", ("pew", "head", 2))
                    for cc, (at, at_rope) in enumerate(Q_AT):
                        uu = (h + 1) * NC + cc
                        if s == at_rope and h == 1:
                            yield from task(q_rope, uu)
                        if s == at:
                            yield from task(q_latent, uu)
                            if h == 0:
                                yield q_rope_second, uu
                    if s == 30:
                        yield w_o, h + 1
                        yield from task(wv_transpose, h + 1)
                        if not last:
                            yield load, "q", h + 2, ("free", ("wos", "head", h + 1))
                            yield load_kv, h + 2
            yield from late
            if last:
                yield denominators, u
                for t in range(QT):
                    yield head_output, u, t

        whos = ("pe", "act", "dve", "pool", "sp")
        parts = {"pre": prologue(), "body": slots(FIRST[1], BT + FIRST[1]),
                 "last": slots(FIRST[1], BT, True)}
        parts = {part: [(x[0].split(), *x[1:]) if isinstance(x[0], str) else (whos, *x) for x in steps]
                 for part, steps in parts.items()}

        def run(e, who, part, it):
            cn.begin(part, it)
            misc["n"] = {"pre": 0, "body": start["body"], "last": start["last"]}[part]
            prev["v"] = {"pre": [None] * 4, "body": tail["body"], "last": tail["last"]}[part][:]
            for whom, step, *args in parts[part]:
                if who in whom:
                    step(e, who, *args)

        start, tail = {"body": 0, "last": 0}, {"body": [None, None], "last": [None, None]}
        for part in ("pre", "body", "last"):
            for who in whos:
                run(Silent(), who, part, 0)
                if who == "pe":
                    used, users = misc["n"], prev["v"]
            if part == "pre":
                start["body"] = 0
            if part == "body":
                assert (used - start["body"]) % 2 == 0
                start["last"] = start["body"]
                past = [(k[0], k[1], k[2] - PERIOD[k[1]]) + tuple(k[3:]) for k in users]
                tail["body"] = tail["last"] = past
        cn.dry = False

        block = ctx.enter_context(nc.Block())
        owner = {"pe": "S G PV M", "act": "exp hi Ph", "dve": "sum max free", "pool": "Pl pool",
                 "sp": " ".join(n for n in names if n.startswith("d_"))}

        def whole(e, who):
            cn.own = idle["sp"] if who == "sp" else None
            for s in owner[who].split():
                if cn.bias(s):
                    e.sem_inc(sems[s], cn.bias(s))
            run(e, who, "pre", 0)
            cn.wait_all(e, "pre")
            with e.Fori(0, NB - 1) as it:
                run(e, who, "body", it)
            run(e, who, "last", NB - 1)

        @block.tensor
        def _(e):
            whole(e, "pe")

        @block.scalar
        def _(e):
            whole(e, "act")

        @block.vector
        def _(e):
            whole(e, "dve")

        @block.gpsimd
        def _(e):
            whole(e, "pool")

        @block.sync
        def _(e):
            whole(e, "sp")
            cn.wait_all(e, "last")


def rope_tables():
    inv = (1.0 / np.float32(10000.0) ** (np.arange(0, ROPE, 2, dtype=np.float32) / np.float32(ROPE)))
    ang = (np.arange(S, dtype=np.float32)[:, None] * inv.astype(np.float32)).astype(np.float32)
    cos, sin = np.cos(ang), np.sin(ang)
    by_row = np.empty((P, 2, S), np.float32)
    by_row[:, 0] = np.tile(cos.T, (4, 1))
    by_row[:, 1] = np.concatenate([-sin.T, -sin.T, sin.T, sin.T])
    by_pos = np.stack([cos, sin], 1).reshape(NT, P, 2, HALF).transpose(1, 0, 2, 3)
    return by_row, np.ascontiguousarray(by_pos)


def kernel(L0_attn_x, L0_attn_wq, L0_attn_wkv_a, L0_attn_wkv_b, L0_attn_wo, L0_attn_kv_norm_scale,
           L0_ffn_factors, L0_ffn_bias):
    import concourse.bacc as bacc
    from concourse.bass_utils import run_bass_kernel_spmd

    rope_t, rope_n = rope_tables()
    arrays = {"x": np.ascontiguousarray(L0_attn_x).reshape(S, E), "wq": L0_attn_wq, "wkv_a": L0_attn_wkv_a,
              "wkv_b": L0_attn_wkv_b, "wo": L0_attn_wo, "kvs": L0_attn_kv_norm_scale,
              "factors": L0_ffn_factors, "bias": L0_ffn_bias, "rope_t": rope_t, "rope_n": rope_n}
    arrays = {n: np.ascontiguousarray(a) for n, a in arrays.items()}
    nc = bacc.Bacc("TRN2", target_bir_lowering=False, num_devices=1,
                   dynamic_dma_scratch_size=1024)
    ins = [nc.dram_tensor(n + "_in", a.shape, F32, kind="ExternalInput").ap() for n, a in arrays.items()]
    out = nc.dram_tensor("layer_out", (S, E), F32, kind="ExternalOutput").ap()
    build(nc, *ins, out)
    r = run_bass_kernel_spmd(nc, [{n + "_in": a for n, a in arrays.items()}], core_ids=[0])
    return r.results[0]["layer_out"].reshape(1, S, E)
```
